# Optimizing a Trainium2 kernel written in Bass

```python
import numpy as np
import jax
import jax.numpy as jnp

def _softmax(x, axis=-1):
    return jax.nn.softmax(x, axis=axis)

def _gelu(x):
    return jax.nn.gelu(x, approximate=True)

def _silu(x):
    return jax.nn.silu(x)

def _sigmoid(x):
    return jax.nn.sigmoid(x)

def _layernorm(x, axis=-1, eps=1e-05):
    m = jnp.mean(x, axis=axis, keepdims=True)
    v = jnp.var(x, axis=axis, keepdims=True)
    return (x - m) / jnp.sqrt(v + eps)

def _scatter_add(tgt, idx, src, axis=0):
    return tgt.at[idx].add(src)

def _segment_sum(src, seg, n):
    return jax.ops.segment_sum(src, seg, n)
kernel_name = 'mk_gnn_resnorm_d2_gnn_r8_38cfb3'

def setup_inputs(seed: int=0):
    np.random.seed(seed)
    _w = jnp.asarray

    def _rec_inputs():
        import jax
        import jax.numpy as jnp
        _gk = jax.random.key(seed)
        x = -0.0005121 + 1.001 * jax.random.normal(jax.random.fold_in(_gk, 1), (12500, 64), jnp.float32)
        src = jax.random.randint(jax.random.fold_in(_gk, 2), (400000,), 0, 12500, jnp.int32)
        dst = jax.random.randint(jax.random.fold_in(_gk, 3), (400000,), 0, 12500, jnp.int32)
        _o = jnp.argsort(dst, stable=True)
        src = src[_o]
        dst = dst[_o]
        edge_attr_64 = -9.77346e-05 + 0.999888 * jax.random.normal(jax.random.fold_in(_gk, 12), (400000, 64), jnp.float32)
        edge_type_8 = jax.random.randint(jax.random.fold_in(_gk, 13), (400000,), 0, 8, jnp.int32)
        edge_weight = jax.random.uniform(jax.random.fold_in(_gk, 14), (400000,), jnp.float32, 0.0, 1)
        return (x, src, dst, edge_attr_64, edge_type_8, edge_weight)
    x, src, dst, edge_attr_64, edge_type_8, edge_weight = _rec_inputs()

    def _L0_gnn_setup():
        import jax, jax.numpy as jnp
        import numpy as np
        N = 6250
        E = 100000
        H = 64
        R = 2

        def _gru_cell(x, h, w_ih, b_ih, w_hh, b_hh):
            gi = x @ w_ih.T + b_ih
            gh = h @ w_hh.T + b_hh
            i_r, i_z, i_n = jnp.split(gi, 3, axis=1)
            h_r, h_z, h_n = jnp.split(gh, 3, axis=1)
            r = jax.nn.sigmoid(i_r + h_r)
            z = jax.nn.sigmoid(i_z + h_z)
            n = jnp.tanh(i_n + r * h_n)
            return (1.0 - z) * n + z * h
        key = jax.random.key(seed)
        ks = jax.random.split(key, 10)
        s = 1.0 / np.sqrt(H)
        return {'hv': jax.random.normal(ks[0], (N, H), jnp.float32), 'he': jax.random.normal(ks[1], (E, H), jnp.float32), 'src': jax.random.randint(ks[2], (E,), 0, N, jnp.int32), 'dst': jax.random.randint(ks[3], (E,), 0, N, jnp.int32), 'w_msg': jax.random.uniform(ks[4], (R, 2 * H, 3 * H), jnp.float32, -s, s), 'b_msg': jax.random.uniform(ks[5], (R, 2 * H), jnp.float32, -s, s), 'w_ih': jax.random.uniform(ks[6], (R, 3 * H, 2 * H), jnp.float32, -s, s), 'w_hh': jax.random.uniform(ks[7], (R, 3 * H, H), jnp.float32, -s, s), 'b_ih': jax.random.uniform(ks[8], (R, 3 * H), jnp.float32, -s, s), 'b_hh': jax.random.uniform(ks[9], (R, 3 * H), jnp.float32, -s, s)}
    _L0_gnn_all = _L0_gnn_setup()
    _L0_gnn_in = {k: v for k, v in _L0_gnn_all.items() if k in ('w_msg', 'b_msg', 'w_ih', 'w_hh', 'b_ih', 'b_hh')}
    del _L0_gnn_all

    def _L1_gnn_setup():
        import jax, jax.numpy as jnp
        import numpy as np
        N_NODES = 12500
        N_EDGES = 400000
        N_RELS = 8
        F_IN = 64
        F_OUT = 64
        key = jax.random.key(seed)
        k1, k2, k3, k4, k5, k6 = jax.random.split(key, 6)
        X = jax.random.normal(k1, (N_NODES, F_IN), dtype=jnp.float32)
        W = jax.random.normal(k2, (N_RELS, F_IN, F_OUT), dtype=jnp.float32) * 0.1
        A = jax.random.uniform(k3, (N_EDGES,), dtype=jnp.float32)
        src = jax.random.randint(k4, (N_EDGES,), 0, N_NODES, dtype=jnp.int32)
        dst = jax.random.randint(k5, (N_EDGES,), 0, N_NODES, dtype=jnp.int32)
        etype = jax.random.randint(k6, (N_EDGES,), 0, N_RELS, dtype=jnp.int32)
        return {'X': X, 'W': W, 'A': A, 'src': src, 'dst': dst, 'etype': etype}
    _L1_gnn_all = _L1_gnn_setup()
    _L1_gnn_in = {k: v for k, v in _L1_gnn_all.items() if k in ('W',)}
    del _L1_gnn_all
    return {'x': x, 'src': src, 'dst': dst, 'edge_attr_64': edge_attr_64, 'edge_type_8': edge_type_8, 'edge_weight': edge_weight, 'L0_gnn_w_msg': _L0_gnn_in['w_msg'], 'L0_gnn_b_msg': _L0_gnn_in['b_msg'], 'L0_gnn_w_ih': _L0_gnn_in['w_ih'], 'L0_gnn_w_hh': _L0_gnn_in['w_hh'], 'L0_gnn_b_ih': _L0_gnn_in['b_ih'], 'L0_gnn_b_hh': _L0_gnn_in['b_hh'], 'L1_gnn_W': _L1_gnn_in['W']}

def reference(x, src, dst, edge_attr_64, edge_type_8, edge_weight, L0_gnn_w_msg, L0_gnn_b_msg, L0_gnn_w_ih, L0_gnn_w_hh, L0_gnn_b_ih, L0_gnn_b_hh, L1_gnn_W):
    import jax
    import jax.numpy as jnp

    def _L0_gnn_ref(hv, he, src, dst, w_msg, b_msg, w_ih, w_hh, b_ih, b_hh):
        import jax, jax.numpy as jnp
        import numpy as np
        N = 6250
        E = 100000
        H = 64
        R = 2

        def _gru_cell(x, h, w_ih, b_ih, w_hh, b_hh):
            gi = x @ w_ih.T + b_ih
            gh = h @ w_hh.T + b_hh
            i_r, i_z, i_n = jnp.split(gi, 3, axis=1)
            h_r, h_z, h_n = jnp.split(gh, 3, axis=1)
            r = jax.nn.sigmoid(i_r + h_r)
            z = jax.nn.sigmoid(i_z + h_z)
            n = jnp.tanh(i_n + r * h_n)
            return (1.0 - z) * n + z * h
        n_nodes = hv.shape[0]
        for t in range(R):
            msg_in = jnp.concatenate([hv[dst], hv[src], he], axis=1)
            e_act = msg_in @ w_msg[t].T + b_msg[t]
            a = jax.ops.segment_sum(e_act, dst, num_segments=n_nodes)
            hv = _gru_cell(a, hv, w_ih[t], b_ih[t], w_hh[t], b_hh[t])
        return hv

    def _L1_gnn_ref(X, W, A, src, dst, etype):
        import jax, jax.numpy as jnp
        import numpy as np
        N_NODES = 12500
        N_EDGES = 400000
        N_RELS = 8
        F_IN = 64
        F_OUT = 64
        XW = jnp.einsum('nf,rfo->rno', X, W)
        msg = XW[etype, src] * A[:, None]
        Y = jax.ops.segment_sum(msg, dst, num_segments=X.shape[0])
        return Y
    x = _layernorm(x + _L0_gnn_ref(x, edge_attr_64, src, dst, L0_gnn_w_msg, L0_gnn_b_msg, L0_gnn_w_ih, L0_gnn_w_hh, L0_gnn_b_ih, L0_gnn_b_hh), axis=-1)
    x = _layernorm(x + _L1_gnn_ref(x, L1_gnn_W, edge_weight, src, dst, edge_type_8), axis=-1)
    return x

_drawn_inputs = setup_inputs


def setup_inputs(seed=0):
    import zlib

    import numpy as np

    out = dict(_drawn_inputs(seed))
    spreads = {}
    factors = {'L0_gnn_b_ih': 2.925, 'L0_gnn_b_hh': 3.268}
    for name, (base, spread) in spreads.items():
        noise = np.random.default_rng([zlib.crc32(name.encode()), seed]).standard_normal(out[name].shape)
        drawn = base * np.exp(spread * noise) if base else spread * noise
        out[name] = jnp.asarray(drawn.astype(out[name].dtype))
    for name, factor in factors.items():
        out[name] = (out[name] * factor).astype(out[name].dtype)
    return out
```

```python
from contextlib import ExitStack

import concourse.bass as bass
from concourse import mybir

F32 = mybir.dt.float32
I32 = mybir.dt.int32
ALU = mybir.AluOpType
ACT = mybir.ActivationFunctionType
AX = mybir.AxisListType

P = 128
G = 25
SLOTS = 5
W = 66
C = 500
CP, CJ = 125, 4
EPS = 1e-5
FREE = 1


def gnn_program(nc, x, xT, src, dst, etype, eweight, he, w_msg_edge, w_msg_dst, w_ihT, w_hhT, b_ih, b_hh, w_rel, out):
    N, H = x.shape
    E = he.shape[0]
    ROUNDS = w_ihT.shape[0]
    RELS = w_rel.shape[1] // H
    NG = E // (P * G)
    ITERS = NG // SLOTS
    CHUNKS = N // C
    NW = N + P
    PASSES = ROUNDS + 1
    assert NG * P * G == E and ITERS * SLOTS == NG and CHUNKS * C == N and H == 64 and CP * CJ == C

    he_v = he.rearrange("(g p t) f -> g p (t f)", p=P, t=G)
    x_v = x.rearrange("(c p j) f -> c p (j f)", p=CP, j=CJ)
    out_v = out.rearrange("(c p j) f -> c p (j f)", p=CP, j=CJ)
    hv_d = nc.dram_tensor("hv_d", [N, H], F32).ap()
    y_d = nc.dram_tensor("y_d", [N, H], F32).ap()
    xw_d = nc.dram_tensor("xw_d", [N * RELS, H], F32).ap()
    relidx_d = nc.dram_tensor("relidx_d", [P, NG * G], I32).ap()
    hv_v = hv_d.rearrange("(c p j) f -> c p (j f)", p=CP, j=CJ)
    y_v = y_d.rearrange("(c p j) f -> c p (j f)", p=CP, j=CJ)
    xw_v = xw_d.rearrange("(c p j r) f -> c p (j r f)", p=CP, j=CJ, r=RELS)

    ctx = ExitStack()
    with ctx:
        def sb(name, shape, dt=F32):
            return ctx.enter_context(nc.sbuf_tensor(name, shape, dt))

        def ps(name):
            return ctx.enter_context(nc.psum_tensor(name, [P, 512], F32))

        def sem(name):
            return ctx.enter_context(nc.semaphore(name))

        sums = sb("sums", [P, NW])
        nodes = sb("nodes", [H + 1, NW])
        srcidx = sb("srcidx", [P, NG, G], I32)
        dstrel = sb("dstrel", [P, NG, G])
        ewt = sb("ewt", [P, NG, G])
        msg = sb("msg", [P, SLOTS, G, W])
        he_t = sb("he_t", [P, 2, G * H])
        onehot = sb("onehot", [P, G, P])
        idx_now = sb("idx_now", [P, SLOTS, G], I32)
        dst_now = sb("dst_now", [P, G])
        ewt_now = sb("ewt_now", [P, G])
        iota = sb("iota", [P, P])
        ident = sb("ident", [P, P])
        ones = sb("ones", [P, P])
        sel_deg = sb("sel_deg", [H + 1, H])
        lim = sb("lim", [P, 2, NG])
        limT = sb("limT", [NG, 2])
        diag = sb("diag", [NG, 2, NG])
        plan = sb("plan", [P, 3, NG], I32)
        wm_edge = sb("wm_edge", [P, ROUNDS, P])
        wm_dst = sb("wm_dst", [H + 1, ROUNDS, P])
        wih = sb("wih", [P, ROUNDS, 3 * H])
        whh = sb("whh", [H + 1, ROUNDS, 3 * H])
        bih = sb("bih", [H, ROUNDS, 3])
        bhh = sb("bhh", [H, ROUNDS, 3])
        brz = sb("brz", [H, ROUNDS, 2])
        wrel = sb("wrel", [H, RELS * H])
        eps = sb("eps", [P, 1])
        stat = sb("stat", [P, 3, CJ])

        flat = msg[:, :, :, :].rearrange("p s t w -> p (s t w)")
        xw_t = flat[:, 0:CJ * RELS * H]
        o = CJ * RELS * H
        area = [flat[:, o + n * 512:o + n * 512 + C] for n in range(10)]
        dh, a_t, r_t, z_t, n_t, t_t, hn_t, yT_t = area[0:8]
        assert o + 10 * 512 <= SLOTS * G * W
        nm = area[8][:, 0:CJ * H]
        sq = area[9][:, 0:CJ * H]
        x_t = he_t[:, 0, 0:CJ * H]
        type_t = he_t[:, :, :].rearrange("p a b -> p (a b)").bitcast(I32)[:, 0:NG * G]
        dsti = onehot[:, :, :].rearrange("p a b -> p (a b)").bitcast(I32)[:, 0:NG * G]
        relf = flat[:, 0:NG * G]
        relidx = flat[:, NG * G:2 * NG * G].bitcast(I32)

        pS, pH, pA, pR, pZ, pN, pM, pT = [ps(n) for n in ("pS", "pH", "pA", "pR", "pZ", "pN", "pM", "pT")]

        const_in = sem("const_in")
        src_in = sem("src_in")
        dst_in = sem("dst_in")
        type_in = sem("type_in")
        iota_made = sem("iota_made")
        memory_set = sem("memory_set")
        lims_found = sem("lims_found")
        lims_turned = sem("lims_turned")
        diag_made = sem("diag_made")
        lims_spread = sem("lims_spread")
        plan_made = sem("plan_made")
        dve_step = sem("dve_step")
        relidx_made = sem("relidx_made")
        relidx_out = sem("relidx_out")
        relidx_in = sem("relidx_in")
        he_in = [sem(f"he_in{n}") for n in range(2)]
        idx_staged = sem("idx_staged")
        gathered = [sem(f"gathered{n}") for n in range(SLOTS)]
        slot_free = [sem(f"slot_free{n}") for n in range(PASSES)]
        onehots_ready = [sem(f"onehots_ready{n}") for n in range(PASSES)]
        window_summed = [sem(f"window_summed{n}") for n in range(PASSES)]
        pass_done = sem("pass_done")
        deg_spread = sem("deg_spread")
        dh_made = sem("dh_made")
        a_made = sem("a_made")
        a_copied = sem("a_copied")
        gates_made = sem("gates_made")
        rz_made = sem("rz_made")
        n_arg_made = sem("n_arg_made")
        n_made = sem("n_made")
        hn_made = sem("hn_made")
        hv_kept = sem("hv_kept")
        hn_turned = sem("hn_turned")
        rows_made = sem("rows_made")
        rows_out = sem("rows_out")
        x_in = sem("x_in")
        var_made = sem("var_made")
        sd_made = sem("sd_made")
        y_made = sem("y_made")
        y_turned = sem("y_turned")
        yT_made = sem("yT_made")
        xw_made = sem("xw_made")
        xw_copied = sem("xw_copied")
        xw_out = sem("xw_out")
        y_in = sem("y_in")
        yt_copied = sem("yt_copied")
        yt_turned = sem("yt_turned")
        fin_made = sem("fin_made")
        fin_out = sem("fin_out")
        nm_free = sem("nm_free")
        xw_free = sem("xw_free")
        wait_over = sem("wait_over")

        block = ctx.enter_context(nc.Block())

        @block.sync
        def _(sp):
            for free in (a_made, yT_made, rows_made, xw_copied, y_made, fin_made, yt_turned, nm_free, xw_free):
                sp.sem_inc(free, FREE)
            sp.dma_start(dsti, dst).then_inc(dst_in, 16)
            sp.dma_start(srcidx[:, :, :].rearrange("p a b -> p (a b)"), src).then_inc(src_in, 16)
            sp.dma_start(type_t, etype).then_inc(type_in, 16)
            sp.dma_start(ewt[:, :, :].rearrange("p a b -> p (a b)"), eweight).then_inc(const_in, 16)
            sp.dma_start(nodes[0:H, 0:N], xT).then_inc(const_in, 16)
            sp.dma_start(wm_edge[:, :, :], w_msg_edge.rearrange("r k m -> k r m")).then_inc(const_in, 16)
            sp.dma_start(wm_dst[:, :, :], w_msg_dst.rearrange("r k m -> k r m")).then_inc(const_in, 16)
            sp.dma_start(wih[:, :, :], w_ihT.rearrange("r k m -> k r m")).then_inc(const_in, 16)
            sp.dma_start(whh[0:H, :, :], w_hhT.rearrange("r k m -> k r m")).then_inc(const_in, 16)
            sp.dma_start(bih[:, :, :], b_ih).then_inc(const_in, 16)
            sp.dma_start(bhh[:, :, :], b_hh).then_inc(const_in, 16)
            sp.dma_start(wrel[:, :], w_rel).then_inc(const_in, 16)
            sp.wait_ge(relidx_made, 1)
            sp.dma_start(relidx_d, relidx).then_inc(relidx_out, 16)
            with sp.Fori(0, ITERS) as i:
                for s in range(SLOTS):
                    sp.wait_ge(slot_free[0], i * SLOTS + (SLOTS + s - (1 if s != 1 else 2)
                                                          + (1 if s == 0 else 0)))
                    sp.sem_inc(wait_over, 1)
                    sp.dma_start(he_t[:, s % 2, :],
                                 he_v[bass.ds(i * SLOTS + s, 1), :, :].rearrange("a p f -> p (a f)"))\
                      .then_inc(he_in[s % 2], 16)
            for r in range(ROUNDS):
                last = r == ROUNDS - 1
                if last:
                    sp.wait_ge(idx_staged, (r + 1) * NG)
                    sp.wait_ge(relidx_out, 16)
                    sp.dma_start(srcidx[:, :, :].rearrange("p a b -> p (a b)"), relidx_d).then_inc(relidx_in, 16)
                    sp.wait_ge(pass_done, r + 1)
                with sp.Fori(0, CHUNKS) as c:
                    if last:
                        sp.wait_ge(y_made, c + FREE)
                        sp.sem_inc(wait_over, 1)
                        sp.dma_start(x_t[0:CP, :], x_v[bass.ds(c, 1), :, :].rearrange("a p f -> p (a f)"))\
                          .then_inc(x_in, 16)
                        sp.wait_ge(y_made, c + 1 + FREE)
                        sp.sem_inc(wait_over, 1)
                        sp.dma_start(y_v[bass.ds(c, 1), :, :].rearrange("a p f -> p (a f)"), nm[0:CP, :])\
                          .then_inc(rows_out, 16)
                        sp.wait_ge(xw_copied, c * CJ + CJ + FREE)
                        sp.sem_inc(wait_over, 1)
                        sp.dma_start(xw_v[bass.ds(c, 1), :, :].rearrange("a p f -> p (a f)"), xw_t[0:CP, :])\
                          .then_inc(xw_out, 16)
                        sp.wait_ge(rows_out, c * 16 + (16 * (r * CHUNKS + 1)))
                        sp.sem_inc(nm_free, 1)
                        sp.wait_ge(xw_out, c * 16 + 16)
                        sp.sem_inc(xw_free, 1)
                    else:
                        sp.wait_ge(rows_made, c + 1 + FREE)
                        sp.sem_inc(wait_over, 1)
                        sp.dma_start(hv_v[bass.ds(c, 1), :, :].rearrange("a p f -> p (a f)"), nm[0:CP, :])\
                          .then_inc(rows_out, 16)
                        sp.wait_ge(rows_out, c * 16 + (16 * (r * CHUNKS + 1)))
                        sp.sem_inc(nm_free, 1)
            sp.wait_ge(pass_done, PASSES)
            with sp.Fori(0, CHUNKS) as c:
                sp.wait_ge(fin_made, c + FREE)
                sp.sem_inc(wait_over, 1)
                sp.dma_start(x_t[0:CP, :], y_v[bass.ds(c, 1), :, :].rearrange("a p f -> p (a f)"))\
                  .then_inc(y_in, 16)
                sp.wait_ge(fin_made, c + 1 + FREE)
                sp.sem_inc(wait_over, 1)
                sp.dma_start(out_v[bass.ds(c, 1), :, :].rearrange("a p f -> p (a f)"), nm[0:CP, :])\
                  .then_inc(fin_out, 16)
                sp.wait_ge(fin_out, c * 16 + 16)
                sp.sem_inc(nm_free, 1)
            sp.wait_ge(fin_out, 16 * CHUNKS)

        @block.gpsimd
        def _(pool):
            pool.iota(iota[:, :], [[1, P]], base=0, channel_multiplier=0,
                      allow_small_or_imprecise_dtypes=True).then_inc(iota_made, 1)
            pool.memset(ident[:, :], 0.0).then_inc(iota_made, 1)
            pool.wait_ge(iota_made, 2)
            pool.affine_select(out=ident[:, :], in_=ident[:, :], compare_op=ALU.not_equal, fill=1.0,
                               base=0, pattern=[[-1, P]], channel_multiplier=1).then_inc(iota_made, 1)
            pool.memset(ones[:, :], 1.0).then_inc(iota_made, 1)
            for p in range(PASSES):
                table = (x, hv_d, xw_d)[p]
                if p > 0:
                    pool.wait_ge(rows_out, 16 * CHUNKS * p)
                if p == ROUNDS:
                    pool.wait_ge(xw_out, 16 * CHUNKS)
                with pool.Fori(0, ITERS) as i:
                    for s in range(SLOTS):
                        pool.wait_ge(idx_staged, i * SLOTS + (p * NG + s + 1))
                        pool.sem_inc(wait_over, 1)
                        pool.wait_ge(slot_free[p], i * SLOTS + (s + 1))
                        pool.sem_inc(wait_over, 1)
                        for t in range(G):
                            pool.indirect_dma_start(
                                msg[:, s, t, 0:H], None, table,
                                bass.IndirectOffsetOnAxis(idx_now[:, s, t:t + 1], 0)).then_inc(gathered[s], 16)

        @block.scalar
        def _(act):
            for p in range(PASSES):
                if p == 0:
                    act.wait_ge(src_in, 16)
                if p == ROUNDS:
                    act.wait_ge(relidx_in, 16)
                with act.Fori(0, ITERS) as i:
                    for s in range(SLOTS):
                        act.wait_ge(slot_free[p], i * SLOTS + (s + 1))
                        nc.scalar.copy(idx_now[:, s, :],
                                       srcidx[:, bass.ds(i * SLOTS + s, 1), :].rearrange("p a t -> p (a t)"))\
                          .then_inc(idx_staged, 1)
                if p == ROUNDS:
                    break
                last = p == ROUNDS - 1
                act.wait_ge(pass_done, p + 1)
                with act.Fori(0, CHUNKS) as c:
                    cs = bass.ds(c * C, C)
                    n = p * CHUNKS
                    act.wait_ge(a_made, c + (n + FREE))
                    nc.scalar.copy(dh[H:H + 1, :], nodes[H:H + 1, cs]).then_inc(dh_made, 1)
                    act.wait_ge(a_made, c + (n + 1 + FREE))
                    nc.scalar.copy(a_t[:, :], pA[:, 0:C]).then_inc(a_copied, 1)
                    act.wait_ge(gates_made, c + (n + 1))
                    nc.scalar.activation(r_t[0:H, :], pR[0:H, 0:C], ACT.Sigmoid, bias=brz[:, p, 0:1]).then_inc(rz_made, 1)
                    nc.scalar.activation(z_t[0:H, :], pZ[0:H, 0:C], ACT.Sigmoid, bias=brz[:, p, 1:2]).then_inc(rz_made, 1)
                    act.wait_ge(n_arg_made, c + (n + 1))
                    nc.scalar.activation(n_t[0:H, :], t_t[0:H, :], ACT.Tanh, bias=bih[:, p, 2:3]).then_inc(n_made, 1)
                    if not last:
                        act.wait_ge(hn_made, c + (n + 1))
                        nc.scalar.copy(nodes[0:H, cs], hn_t[0:H, :]).then_inc(hv_kept, 1)
                    else:
                        act.wait_ge(var_made, c + 1)
                        nc.scalar.activation(stat[0:CP, 2, :], stat[0:CP, 1, :], ACT.Sqrt, scale=1.0 / H,
                                             bias=eps[0:CP, :]).then_inc(sd_made, 1)
                        act.wait_ge(y_turned, c + 1)
                        nc.scalar.copy(yT_t[0:H, :], pT[0:H, 0:C]).then_inc(yT_made, 1)
                        act.wait_ge(xw_free, c + FREE)
                        act.sem_inc(wait_over, 1)
                        for j in range(CJ):
                            act.wait_ge(xw_made, c * CJ + (j + 1))
                            nc.scalar.copy(xw_t[0:CP, j * RELS * H:(j + 1) * RELS * H], (pR, pZ, pN, pM)[j][0:CP, :])\
                              .then_inc(xw_copied, 1)
            act.wait_ge(pass_done, PASSES)
            with act.Fori(0, CHUNKS) as c:
                cs = bass.ds(c * C, C)
                act.wait_ge(yt_turned, c + FREE)
                nc.scalar.copy(yT_t[0:H, :], sums[0:H, cs]).then_inc(yt_copied, 1)
                act.wait_ge(var_made, c + (CHUNKS + 1))
                nc.scalar.activation(stat[0:CP, 2, :], stat[0:CP, 1, :], ACT.Sqrt, scale=1.0 / H,
                                     bias=eps[0:CP, :]).then_inc(sd_made, 1)

        @block.tensor
        def _(pe):
            pe.wait_ge(iota_made, 4)
            pe.wait_ge(lims_found, 2)
            nc.tensor.transpose(pS[0:NG, 0:P], lim[:, 0, :], ident[:, :]).then_inc(lims_turned, 1)
            nc.tensor.transpose(pS[0:NG, P:2 * P], lim[:, 1, :], ident[:, :]).then_inc(lims_turned, 1)
            pe.wait_ge(diag_made, 2)
            nc.tensor.matmul(pH[:, 0:2 * NG], ones[0:NG, :], diag[:, :, :].rearrange("p a b -> p (a b)"),
                             start=True, stop=True).then_inc(lims_spread, 1)
            pe.wait_ge(plan_made, 3)
            pe.wait_ge(memory_set, 6)
            pe.wait_ge(const_in, 16 * 9)
            for p in range(PASSES):
                with pe.Fori(0, ITERS) as i:
                    for s in range(SLOTS):
                        g = i * SLOTS + s
                        windows = pe.value_load(plan[0:1, 1, bass.ds(g, 1)], min_val=1, max_val=P)
                        before = pe.value_load(plan[0:1, 2, bass.ds(g, 1)], min_val=0, max_val=NG * P)
                        pe.wait_ge(gathered[s], i * (16 * G) + (p * 16 * G * ITERS + 16 * G))
                        pe.sem_inc(wait_over, 1)
                        if p == 0:
                            pe.wait_ge(he_in[s % 2], i * (48 if s % 2 == 0 else 32) + 16 * (s // 2 + 1))
                            pe.sem_inc(wait_over, 1)
                        with pe.Fori(0, windows) as w:
                            pe.wait_ge(onehots_ready[p], before + w + 1)
                            pe.sem_inc(wait_over, 1)
                            for t in range(G):
                                last = nc.tensor.matmul(pS[0:H + 1, 0:P], msg[:, s, t, 0:H + 1], onehot[:, t, :],
                                                        start=t == 0, stop=t == G - 1)
                            if p == 0:
                                for t in range(G):
                                    last = nc.tensor.matmul(pH[H:2 * H, 0:P], he_t[:, s % 2, t * H:(t + 1) * H],
                                                            onehot[:, t, :], start=t == 0, stop=t == G - 1)
                            last.then_inc(window_summed[p], 1)
                if p == ROUNDS:
                    break
                last_round = p == ROUNDS - 1
                pe.wait_ge(pass_done, p + 1)
                with pe.Fori(0, CHUNKS) as c:
                    cs = bass.ds(c * C, C)
                    n = p * CHUNKS
                    if last_round:
                        pe.wait_ge(yT_made, c + FREE)
                    else:
                        pe.wait_ge(rows_made, c + FREE)
                    pe.sem_inc(wait_over, 1)
                    nc.tensor.matmul(pS[0:H, 0:C], sel_deg[:, :], nodes[:, cs], start=True, stop=True)\
                      .then_inc(deg_spread, 1)
                    nc.tensor.matmul(pA[:, 0:C], wm_edge[:, p, :], sums[:, cs], start=True, stop=False)
                    pe.wait_ge(dh_made, c * 2 + (2 * n + 2))
                    pe.sem_inc(wait_over, 1)
                    nc.tensor.matmul(pA[:, 0:C], wm_dst[:, p, :], dh[0:H + 1, :], start=False, stop=True)\
                      .then_inc(a_made, 1)
                    if last_round:
                        pe.wait_ge(xw_copied, c * CJ + FREE)
                        pe.sem_inc(wait_over, 1)
                    nc.tensor.matmul(pM[0:H, 0:C], whh[:, p, 2 * H:3 * H], nodes[:, cs], start=True, stop=True)
                    nc.tensor.matmul(pR[0:H, 0:C], whh[:, p, 0:H], nodes[:, cs], start=True, stop=False)
                    nc.tensor.matmul(pZ[0:H, 0:C], whh[:, p, H:2 * H], nodes[:, cs], start=True, stop=False)
                    pe.wait_ge(a_copied, c + (n + 1))
                    pe.sem_inc(wait_over, 1)
                    nc.tensor.matmul(pR[0:H, 0:C], wih[:, p, 0:H], a_t[:, :], start=False, stop=True)
                    nc.tensor.matmul(pZ[0:H, 0:C], wih[:, p, H:2 * H], a_t[:, :], start=False, stop=True)
                    nc.tensor.matmul(pN[0:H, 0:C], wih[:, p, 2 * H:3 * H], a_t[:, :], start=True, stop=True)\
                      .then_inc(gates_made, 1)
                    pe.wait_ge(hn_made, c + (n + 1))
                    pe.sem_inc(wait_over, 1)
                    hn_rows = hn_t[0:H, :].rearrange("f (p j) -> f j p", j=CJ)
                    for j in range(CJ):
                        turned = nc.tensor.transpose(pT[0:CP, j * H:(j + 1) * H], hn_rows[:, j, :], ident[0:H, 0:H])
                    turned.then_inc(hn_turned, 1)
                    if last_round:
                        pe.wait_ge(y_made, c + 1 + FREE)
                        pe.sem_inc(wait_over, 1)
                        for j in range(CJ):
                            turned = nc.tensor.transpose(pT[0:H, j * CP:(j + 1) * CP], nm[0:CP, j * H:(j + 1) * H],
                                                         ident[0:CP, 0:CP])
                        turned.then_inc(y_turned, 1)
                        pe.wait_ge(yT_made, c + 1 + FREE)
                        pe.sem_inc(wait_over, 1)
                        for j in range(CJ):
                            nc.tensor.matmul((pR, pZ, pN, pM)[j][0:CP, :], yT_t[0:H, j * CP:(j + 1) * CP], wrel[:, :],
                                             start=True, stop=True).then_inc(xw_made, 1)
            with pe.Fori(0, CHUNKS) as c:
                pe.wait_ge(yt_copied, c + 1)
                pe.sem_inc(wait_over, 1)
                pe.wait_ge(fin_made, c + FREE)
                pe.sem_inc(wait_over, 1)
                y_rows = yT_t[0:H, :].rearrange("f (p j) -> f j p", j=CJ)
                for j in range(CJ):
                    turned = nc.tensor.transpose(pT[0:CP, j * H:(j + 1) * H], y_rows[:, j, :], ident[0:H, 0:H])
                turned.then_inc(yt_turned, 1)

        @block.vector
        def _(dve):
            steps = 0

            def chained(instruction):
                nonlocal steps
                steps += 1
                instruction.then_inc(dve_step, 1)
                dve.wait_ge(dve_step, steps)

            nc.vector.memset(sums[:, :], 0.0).then_inc(memory_set, 1)
            nc.vector.memset(nodes[H:H + 1, :], 0.0).then_inc(memory_set, 1)
            nc.vector.memset(sel_deg[0:H, :], 0.0).then_inc(memory_set, 1)
            nc.vector.memset(sel_deg[H:H + 1, :], 1.0).then_inc(memory_set, 1)
            nc.vector.memset(whh[H:H + 1, :, :], 0.0).then_inc(memory_set, 1)
            nc.vector.memset(eps[:, :], EPS)
            dve.wait_ge(dst_in, 16)
            chained(nc.vector.tensor_copy(dstrel[:, :, :].rearrange("p a b -> p (a b)"), dsti))
            nc.vector.tensor_reduce(lim[:, 0, :], dstrel[:, :, :], axis=AX.X, op=ALU.max).then_inc(lims_found, 1)
            nc.vector.tensor_reduce(lim[:, 1, :], dstrel[:, :, :], axis=AX.X, op=ALU.min, negate=True)\
              .then_inc(lims_found, 1)
            dve.wait_ge(src_in, 16)
            chained(nc.vector.tensor_scalar(relf, srcidx[:, :, :].rearrange("p a b -> p (a b)"), float(RELS), None,
                                            op0=ALU.mult))
            dve.wait_ge(type_in, 16)
            nc.vector.tensor_tensor(relidx, relf, type_t, op=ALU.add).then_inc(relidx_made, 1)
            dve.wait_ge(lims_turned, 2)
            chained(nc.vector.tensor_reduce(limT[:, :], pS[0:NG, 0:2 * P].rearrange("p (a b) -> p a b", a=2),
                                            axis=AX.X, op=ALU.max))
            dve.wait_ge(iota_made, 4)
            for a in range(2):
                nc.vector.tensor_scalar(diag[:, a, :], ident[0:NG, 0:NG], limT[:, a:a + 1], None, op0=ALU.mult)\
                  .then_inc(diag_made, 1)
            dve.wait_ge(lims_spread, 1)
            greatest, neg_least = pH[:, 0:NG], pH[:, NG:2 * NG]
            nc.vector.tensor_scalar(plan[:, 0, :], neg_least, -1.0, None, op0=ALU.mult).then_inc(plan_made, 1)
            chained(nc.vector.tensor_copy(lim[:, 0, :], neg_least))
            nc.vector.tensor_tensor(dstrel[:, :, :], dstrel[:, :, :],
                                    lim[:, 0, :].unsqueeze(2).broadcast_to([P, NG, G]), op=ALU.add)
            chained(nc.vector.tensor_tensor(plan[:, 1, :], greatest, lim[:, 0, :], op=ALU.add))
            chained(nc.vector.tensor_scalar(plan[:, 1, :], plan[:, 1, :], 7, None, op0=ALU.arith_shift_right))
            chained(nc.vector.tensor_scalar(lim[:, 1, :], plan[:, 1, :], 1.0, None, op0=ALU.add))
            nc.vector.tensor_copy(plan[:, 1, :], lim[:, 1, :]).then_inc(plan_made, 1)
            chained(nc.vector.tensor_tensor_scan(lim[:, 0, :], ones[:, 0:NG], lim[:, 1, :], initial=0.0,
                                                 op0=ALU.mult, op1=ALU.add))
            nc.vector.tensor_tensor(plan[:, 2, :], lim[:, 0, :], lim[:, 1, :], op=ALU.subtract).then_inc(plan_made, 1)
            dve.wait_ge(plan_made, 3)
            dve.wait_ge(relidx_out, 16)
            dve.wait_ge(const_in, 16 * 9)
            chained(nc.vector.tensor_tensor(brz[:, :, :], bih[:, :, 0:2], bhh[:, :, 0:2], op=ALU.add))
            nc.vector.memset(msg[:, :, :, H:H + 1], 1.0).then_inc(memory_set, 1)

            for p in range(PASSES):
                nc.vector.memset(stat[:, 0, 0:1], 0.0).then_inc(slot_free[p], SLOTS)
                with dve.Fori(0, ITERS) as i:
                    for s in range(SLOTS):
                        g = i * SLOTS + s
                        first = dve.value_load(plan[0:1, 0, bass.ds(g, 1)], min_val=0, max_val=N - 1)
                        windows = dve.value_load(plan[0:1, 1, bass.ds(g, 1)], min_val=1, max_val=P)
                        before = dve.value_load(plan[0:1, 2, bass.ds(g, 1)], min_val=0, max_val=NG * P)
                        nc.vector.tensor_copy(dst_now[:, :], dstrel[:, bass.ds(g, 1), :].rearrange("p a t -> p (a t)"))
                        if p == ROUNDS:
                            nc.vector.tensor_copy(ewt_now[:, :], ewt[:, bass.ds(g, 1), :].rearrange("p a t -> p (a t)"))
                        with dve.Fori(0, windows) as w:
                            dve.drain()
                            for t in range(G):
                                if p == ROUNDS:
                                    made = nc.vector.tensor_scalar(onehot[:, t, :], iota[:, :], dst_now[:, t:t + 1],
                                                                   ewt_now[:, t:t + 1], op0=ALU.is_equal, op1=ALU.mult)
                                else:
                                    made = nc.vector.tensor_scalar(onehot[:, t, :], iota[:, :], dst_now[:, t:t + 1],
                                                                   None, op0=ALU.is_equal)
                            made.then_inc(onehots_ready[p], 1)
                            dve.wait_ge(window_summed[p], before + w + 1)
                            dve.sem_inc(wait_over, 1)
                            dve.drain()
                            nc.vector.tensor_scalar(dst_now[:, :], dst_now[:, :], -float(P), None, op0=ALU.add)
                            span = bass.ds(nc.s_assert_within(first + w * P, min_val=0, max_val=N - 1), P)
                            nc.vector.tensor_tensor(sums[0:H, span], sums[0:H, span], pS[0:H, 0:P], op=ALU.add)
                            if p == 0:
                                nc.vector.tensor_tensor(nodes[H:H + 1, span], nodes[H:H + 1, span],
                                                        pS[H:H + 1, 0:P], op=ALU.add)
                                nc.vector.tensor_tensor(sums[H:2 * H, span], sums[H:2 * H, span],
                                                        pH[H:2 * H, 0:P], op=ALU.add)
                        dve.drain()
                        dve.sem_inc(slot_free[p], 1)
                nc.vector.memset(stat[:, 0, 0:1], 0.0).then_inc(pass_done, 1)
                if p == ROUNDS:
                    break
                last = p == ROUNDS - 1
                with dve.Fori(0, CHUNKS) as c:
                    cs = bass.ds(c * C, C)
                    n = p * CHUNKS
                    dve.wait_ge(a_made, c + (n + FREE))
                    dve.sem_inc(wait_over, 1)
                    dve.wait_ge(deg_spread, c + (n + 1))
                    nc.vector.tensor_tensor(dh[0:H, :], nodes[0:H, cs], pS[0:H, 0:C], op=ALU.mult).then_inc(dh_made, 1)
                    dve.wait_ge(rz_made, c * 2 + (2 * n + 2))
                    nc.vector.scalar_tensor_tensor(t_t[0:H, :], pM[0:H, 0:C], bhh[:, p, 2:3], r_t[0:H, :],
                                                   op0=ALU.add, op1=ALU.mult)
                    dve.drain()
                    nc.vector.tensor_tensor(t_t[0:H, :], t_t[0:H, :], pN[0:H, 0:C], op=ALU.add).then_inc(n_arg_made, 1)
                    dve.wait_ge(n_made, c + (n + 1))
                    nc.vector.tensor_tensor(t_t[0:H, :], nodes[0:H, cs], n_t[0:H, :], op=ALU.subtract)
                    dve.drain()
                    nc.vector.tensor_tensor(t_t[0:H, :], t_t[0:H, :], z_t[0:H, :], op=ALU.mult)
                    dve.drain()
                    nc.vector.tensor_tensor(hn_t[0:H, :], n_t[0:H, :], t_t[0:H, :], op=ALU.add).then_inc(hn_made, 1)
                    dve.wait_ge(nm_free, c + (n + FREE))
                    dve.sem_inc(wait_over, 1)
                    dve.wait_ge(hn_turned, c + (n + 1))
                    if not last:
                        nc.vector.tensor_copy(nm[0:CP, :], pT[0:CP, 0:CJ * H]).then_inc(rows_made, 1)
                    else:
                        dve.sem_inc(wait_over, 1)
                        dve.wait_ge(x_in, c * 16 + 16)
                        nc.vector.tensor_tensor(sq[0:CP, :], x_t[0:CP, :], pT[0:CP, 0:CJ * H], op=ALU.add)
                        dve.drain()
                        norm_rows(nc, dve, sq, nm, stat, var_made, sd_made, c + 1, CP, CJ, H).then_inc(y_made, 1)
                dve.wait_ge(a_made, CHUNKS * (p + 1) + FREE)
                nc.vector.memset(sums[0:H, :], 0.0)
                if not last:
                    dve.wait_ge(hv_kept, CHUNKS)
                else:
                    dve.wait_ge(rows_out, 16 * CHUNKS * ROUNDS)
                    dve.wait_ge(xw_out, 16 * CHUNKS)
            with dve.Fori(0, CHUNKS) as c:
                dve.wait_ge(nm_free, c + (ROUNDS * CHUNKS + FREE))
                dve.sem_inc(wait_over, 1)
                dve.wait_ge(yt_turned, c + 1 + FREE)
                dve.sem_inc(wait_over, 1)
                dve.wait_ge(y_in, c * 16 + 16)
                nc.vector.tensor_tensor(sq[0:CP, :], x_t[0:CP, :], pT[0:CP, 0:CJ * H], op=ALU.add)
                dve.drain()
                norm_rows(nc, dve, sq, nm, stat, var_made, sd_made, c + (CHUNKS + 1), CP, CJ, H).then_inc(fin_made, 1)


def norm_rows(nc, dve, rows, out, stat, var_made, sd_made, count, CP, CJ, H):
    r = rows[0:CP, :].rearrange("p (j f) -> p j f", j=CJ)
    q = out[0:CP, :].rearrange("p (j f) -> p j f", j=CJ)
    mean = stat[0:CP, 0, :]
    nc.vector.tensor_reduce(mean, r, axis=AX.X, op=ALU.add)
    dve.drain()
    nc.vector.tensor_scalar(mean, mean, -1.0 / H, None, op0=ALU.mult)
    dve.drain()
    nc.vector.tensor_tensor(r, r, mean.unsqueeze(2).broadcast_to([CP, CJ, H]), op=ALU.add)
    dve.drain()
    nc.vector.tensor_tensor(q, r, r, op=ALU.mult)
    dve.drain()
    nc.vector.tensor_reduce(stat[0:CP, 1, :], q, axis=AX.X, op=ALU.add).then_inc(var_made, 1)
    dve.wait_ge(sd_made, count)
    nc.vector.reciprocal(mean, stat[0:CP, 2, :])
    dve.drain()
    return nc.vector.tensor_tensor(q, r, mean.unsqueeze(2).broadcast_to([CP, CJ, H]), op=ALU.mult)


def kernel(x, src, dst, edge_attr_64, edge_type_8, edge_weight, L0_gnn_w_msg, L0_gnn_b_msg, L0_gnn_w_ih,
           L0_gnn_w_hh, L0_gnn_b_ih, L0_gnn_b_hh, L1_gnn_W):
    import numpy as np
    import concourse.bacc as bacc
    from concourse.bass_utils import run_bass_kernel_spmd

    R, H3, M = L0_gnn_w_ih.shape
    H = H3 // 3

    def by_partition(a):
        return np.asarray(a).reshape(-1, P, G).transpose(1, 0, 2).reshape(P, -1)

    w_msgT = np.asarray(L0_gnn_w_msg).transpose(0, 2, 1)
    arrays = {
        "x": np.asarray(x),
        "xT": np.asarray(x).T,
        "src": by_partition(src),
        "dst": by_partition(dst),
        "etype": by_partition(edge_type_8),
        "eweight": by_partition(edge_weight),
        "he": np.asarray(edge_attr_64),
        "w_msg_edge": w_msgT[:, H:, :],
        "w_msg_dst": np.concatenate([w_msgT[:, :H, :], np.asarray(L0_gnn_b_msg)[:, None, :]], axis=1),
        "w_ihT": np.asarray(L0_gnn_w_ih).transpose(0, 2, 1),
        "w_hhT": np.asarray(L0_gnn_w_hh).transpose(0, 2, 1),
        "b_ih": np.asarray(L0_gnn_b_ih).reshape(R, 3, H).transpose(2, 0, 1),
        "b_hh": np.asarray(L0_gnn_b_hh).reshape(R, 3, H).transpose(2, 0, 1),
        "w_rel": np.asarray(L1_gnn_W).transpose(1, 0, 2).reshape(H, -1),
    }
    arrays = {f"in_{k}": np.ascontiguousarray(v) for k, v in arrays.items()}
    nc = bacc.Bacc("TRN2", target_bir_lowering=False, num_devices=1)
    args = [nc.dram_tensor(k, v.shape, mybir.dt.from_np(v.dtype), kind="ExternalInput").ap() for k, v in arrays.items()]
    out = nc.dram_tensor("out_rows", np.asarray(x).shape, F32, kind="ExternalOutput").ap()
    gnn_program(nc, *args, out)
    r = run_bass_kernel_spmd(nc, [arrays], core_ids=[0])
    return r.results[0]["out_rows"]
```

```python
from contextlib import ExitStack

import concourse.bass as bass
from concourse import mybir

F32 = mybir.dt.float32
I32 = mybir.dt.int32
ALU = mybir.AluOpType
ACT = mybir.ActivationFunctionType
AX = mybir.AxisListType

P = 128
G = 25
SLOTS = 5
W = 66
C = 500
CP, CJ = 125, 4
PAD = 512
EPS = 1e-5


def wait(eng, sem, value):
    if not isinstance(value, int) or value > 0:
        eng.wait_ge(sem, value)


def chunk_steps(eng, count, depth):
    start = depth + 2
    pairs = (count - start) // 2

    def apart(k):
        return lambda lag: (k - lag, (k - lag) % 2, (k - lag) // 2) if 0 <= k - lag < count else None

    for k in range(start):
        yield apart(k)
    with eng.Fori(0, pairs) as i:
        for k in (start, start + 1):
            yield lambda lag, k=k: (i * 2 + (k - lag), (k - lag) % 2, i + (k - lag) // 2)
    for k in range(start + 2 * pairs, count + depth):
        yield apart(k)


def gnn_program(nc, x, xT, src, dst, etype, eweight, he, w_edge, w_dst, w_node, w_a, w_sel, w_rel, out):
    N, H = x.shape
    E = he.shape[0]
    ROUNDS = w_edge.shape[1]
    RELS = w_rel.shape[1] // H
    NG = E // (P * G)
    ITERS = NG // SLOTS
    CHUNKS = N // C
    EVEN, ODD = (CHUNKS + 1) // 2, CHUNKS // 2
    NW = N + P
    PASSES = ROUNDS + 1
    K_NODE = H + 3
    assert NG * P * G == E and ITERS * SLOTS == NG and CHUNKS * C == N and H == 64 and CP * CJ == C

    he_v = he.rearrange("(g p t) f -> g p (t f)", p=P, t=G)
    x_v = x.rearrange("(c p j) f -> p c (j f)", p=CP, j=CJ)
    out_v = out.rearrange("(c p j) f -> c p (j f)", p=CP, j=CJ)
    hv_d = nc.dram_tensor("hv_d", [N, H], F32).ap()
    y_d = nc.dram_tensor("y_d", [N, H], F32).ap()
    xw_d = nc.dram_tensor("xw_d", [N * RELS, H], F32).ap()
    relidx_d = nc.dram_tensor("relidx_d", [P, NG * G], I32).ap()
    hv_v = hv_d.rearrange("(c p j) f -> c p (j f)", p=CP, j=CJ)
    y_v = y_d.rearrange("(c p j) f -> c p (j f)", p=CP, j=CJ)
    y_all = y_d.rearrange("(c p j) f -> p c (j f)", p=CP, j=CJ)
    xw_v = xw_d.rearrange("(c p j r) f -> c p (j r f)", p=CP, j=CJ, r=RELS)

    ctx = ExitStack()
    with ctx:
        def sb(name, shape, dt=F32):
            return ctx.enter_context(nc.sbuf_tensor(name, shape, dt))

        def ps(name):
            return ctx.enter_context(nc.psum_tensor(name, [P, PAD], F32))

        def sem(name):
            return ctx.enter_context(nc.semaphore(name))

        sums = sb("sums", [P, NW])
        nodes = sb("nodes", [K_NODE, NW])
        srcidx = sb("srcidx", [P, NG * G], I32)
        dstrel = sb("dstrel", [P, NG, G])
        ewt = sb("ewt", [P, NG * G])
        msg = sb("msg", [P, SLOTS, G, W])
        edge_area = sb("edge_area", [P, 2 * G * H + G * P])
        he_t = edge_area[:, 0:2 * G * H].rearrange("p (a f) -> p a f", a=2)
        onehot = edge_area[:, 2 * G * H:].rearrange("p (t n) -> p t n", t=G)
        idx_now = sb("idx_now", [P, SLOTS, G], I32)
        dst_now = sb("dst_now", [P, G])
        ewt_now = sb("ewt_now", [P, G])
        iota = sb("iota", [P, P])
        ident = sb("ident", [P, P])
        ones = sb("ones", [P, P])
        lim = sb("lim", [P, 2, NG])
        limT = sb("limT", [NG, 2])
        diag = sb("diag", [NG, 2, NG])
        plan = sb("plan", [P, 3, NG], I32)
        wedge = sb("wedge", [P, ROUNDS, P])
        wdst = sb("wdst", [H + 1, ROUNDS, P])
        wnode = sb("wnode", [K_NODE, ROUNDS, 2 * P])
        wa = sb("wa", [P, ROUNDS, 2 * P])
        wsel = sb("wsel", [K_NODE, H + 1])
        wrel = sb("wrel", [H, RELS * H])
        eps = sb("eps", [P, 1])
        mean = sb("mean", [P, 2, CJ])
        var = sb("var", [P, 2, CJ])
        std = sb("std", [P, 2, CJ])
        varall = sb("varall", [P, CHUNKS, CJ])
        stdall = sb("stdall", [P, CHUNKS, CJ])

        flat = msg[:, :, :, :].rearrange("p s t w -> p (s t w)")

        def two(at, words):
            return [flat[:, at + n * words:at + (n + 1) * words] for n in range(2)]

        dh, a_t, r_t, z_t, n_t, t_t, hn_t = [two(2 * C * n, C) for n in range(7)]
        nm = two(14 * C, CJ * H)
        sq = two(14 * C + 2 * CJ * H, CJ * H)
        assert 14 * C + 4 * CJ * H <= SLOTS * G * W
        xw_t = two(0, CJ * RELS * H)
        yT_t = two(2 * CJ * RELS * H, C)
        y_t = two(2 * CJ * RELS * H + 2 * C, CJ * H)
        resid = edge_area[:, :].rearrange("p (c j f) -> p c j f", c=CHUNKS, j=CJ)
        relf = sums[:, 0:NG * G]
        relidx = sums[:, NG * G:2 * NG * G].bitcast(I32)
        type_t = sums[:, 2 * NG * G:3 * NG * G].bitcast(I32)
        dsti = sums[:, 3 * NG * G:4 * NG * G].bitcast(I32)

        pS, pH, pD, pA, pR, pN, pT, pY = [ps(n) for n in ("pS", "pH", "pD", "pA", "pR", "pN", "pT", "pY")]
        pX = [pD, pA, pR, pN]

        const_in = sem("const_in")
        nodes_in = sem("nodes_in")
        src_in = sem("src_in")
        dst_in = sem("dst_in")
        type_in = sem("type_in")
        iota_made = sem("iota_made")
        memory_set = sem("memory_set")
        lims_found = sem("lims_found")
        lims_turned = sem("lims_turned")
        diag_made = sem("diag_made")
        lims_spread = sem("lims_spread")
        plan_made = sem("plan_made")
        dve_step = sem("dve_step")
        relidx_made = sem("relidx_made")
        relidx_out = sem("relidx_out")
        relidx_in = sem("relidx_in")
        he_in = [sem(f"he_in{n}") for n in range(2)]
        idx_staged = sem("idx_staged")
        gathered = [sem(f"gathered{n}") for n in range(SLOTS)]
        slot_free = [sem(f"slot_free{n}") for n in range(PASSES)]
        onehots_ready = [sem(f"onehots_ready{n}") for n in range(PASSES)]
        window_summed = [sem(f"window_summed{n}") for n in range(PASSES)]
        pass_done = sem("pass_done")
        deg_spread = sem("deg_spread")
        dh_made = sem("dh_made")
        a_made = sem("a_made")
        a_copied = sem("a_copied")
        gates_made = sem("gates_made")
        rz_made = sem("rz_made")
        n_arg_made = sem("n_arg_made")
        n_made = sem("n_made")
        hn_made = sem("hn_made")
        hv_kept = sem("hv_kept")
        hn_turned = sem("hn_turned")
        rows_read = sem("rows_read")
        rows_out = [sem(f"rows_out{n}") for n in range(2)]
        resid_in = sem("resid_in")
        var_made = sem("var_made")
        std_made = sem("std_made")
        y_made = sem("y_made")
        y_turned = sem("y_turned")
        yT_made = sem("yT_made")
        y_out = [sem(f"y_out{n}") for n in range(2)]
        xw_made = sem("xw_made")
        xw_by_act = sem("xw_by_act")
        xw_by_dve = sem("xw_by_dve")
        xw_out = [sem(f"xw_out{n}") for n in range(2)]
        y_in = sem("y_in")
        sums_copied = sem("sums_copied")
        sums_turned = sem("sums_turned")
        turned_read = sem("turned_read")
        var2_made = sem("var2_made")
        std2_made = sem("std2_made")
        fin_made = sem("fin_made")
        fin_out = [sem(f"fin_out{n}") for n in range(2)]
        wait_over = sem("wait_over")

        def cols(c):
            return bass.ds(c * C, C)

        block = ctx.enter_context(nc.Block())

        @block.sync
        def _(sp):
            sp.dma_start(srcidx[:, :], src).then_inc(src_in, 16)
            sp.dma_start(dsti, dst).then_inc(dst_in, 16)
            sp.dma_start(wedge[:, :, :], w_edge).then_inc(const_in, 16)
            sp.dma_start(wdst[:, :, :], w_dst).then_inc(const_in, 16)
            sp.dma_start(wnode[:, :, :], w_node).then_inc(const_in, 16)
            sp.dma_start(wa[:, :, :], w_a).then_inc(const_in, 16)
            sp.dma_start(wsel[:, :], w_sel).then_inc(const_in, 16)
            sp.dma_start(wrel[:, :], w_rel).then_inc(const_in, 16)
            sp.dma_start(type_t, etype).then_inc(type_in, 16)
            sp.dma_start(ewt[:, :], eweight).then_inc(const_in, 16)
            sp.dma_start(nodes[0:H, 0:N], xT).then_inc(nodes_in, 16)
            sp.wait_ge(relidx_made, 1)
            sp.dma_start(relidx_d, relidx).then_inc(relidx_out, 16)
            with sp.Fori(0, ITERS) as i:
                for s in range(SLOTS):
                    sp.wait_ge(slot_free[0], i * SLOTS + (SLOTS, SLOTS, SLOTS + 1, SLOTS + 2, SLOTS + 3)[s])
                    sp.sem_inc(wait_over, 1)
                    sp.dma_start(he_t[:, s % 2, :],
                                 he_v[bass.ds(i * SLOTS + s, 1), :, :].rearrange("a p f -> p (a f)"))\
                      .then_inc(he_in[s % 2], 16)
            for r in range(ROUNDS - 1):
                sp.wait_ge(pass_done, r + 1)
                for step in chunk_steps(sp, CHUNKS, 0):
                    c, b, h = step(0)
                    sp.wait_ge(rows_read, c + (r * CHUNKS + 1))
                    sp.sem_inc(wait_over, 1)
                    sp.dma_start(hv_v[bass.ds(c, 1), :, :].rearrange("a p f -> p (a f)"), nm[b][0:CP, :])\
                      .then_inc(rows_out[b], 16)
            sp.wait_ge(idx_staged, ROUNDS * NG)
            sp.wait_ge(relidx_out, 16)
            sp.dma_start(srcidx[:, :], relidx_d).then_inc(relidx_in, 16)
            sp.wait_ge(pass_done, ROUNDS)
            sp.dma_start(resid[0:CP, :, :, :].rearrange("p c j f -> p c (j f)"), x_v).then_inc(resid_in, 16)
            for step in chunk_steps(sp, CHUNKS, 1):
                if (k := step(0)):
                    c, b, h = k
                    sp.wait_ge(y_made, c + 1)
                    sp.sem_inc(wait_over, 1)
                    sp.dma_start(y_v[bass.ds(c, 1), :, :].rearrange("a p f -> p (a f)"), y_t[b][0:CP, :])\
                      .then_inc(y_out[b], 16)
                if (k := step(1)):
                    c, b, h = k
                    sp.wait_ge(xw_by_act, c * 2 + 2)
                    sp.sem_inc(wait_over, 1)
                    sp.wait_ge(xw_by_dve, c * 2 + 2)
                    sp.sem_inc(wait_over, 1)
                    sp.dma_start(xw_v[bass.ds(c, 1), :, :].rearrange("a p f -> p (a f)"), xw_t[b][0:CP, :])\
                      .then_inc(xw_out[b], 16)
            sp.wait_ge(pass_done, PASSES)
            sp.wait_ge(y_out[0], 16 * EVEN)
            sp.wait_ge(y_out[1], 16 * ODD)
            sp.dma_start(resid[0:CP, :, :, :].rearrange("p c j f -> p c (j f)"), y_all).then_inc(y_in, 16)
            for step in chunk_steps(sp, CHUNKS, 0):
                c, b, h = step(0)
                sp.wait_ge(fin_made, c + 1)
                sp.sem_inc(wait_over, 1)
                sp.dma_start(out_v[bass.ds(c, 1), :, :].rearrange("a p f -> p (a f)"), nm[b][0:CP, :])\
                  .then_inc(fin_out[b], 16)
            sp.wait_ge(fin_out[0], 16 * EVEN)
            sp.wait_ge(fin_out[1], 16 * ODD)

        @block.gpsimd
        def _(pool):
            pool.iota(iota[:, :], [[1, P]], base=0, channel_multiplier=0,
                      allow_small_or_imprecise_dtypes=True).then_inc(iota_made, 1)
            pool.memset(ident[:, :], 0.0).then_inc(iota_made, 1)
            pool.wait_ge(iota_made, 2)
            pool.affine_select(out=ident[:, :], in_=ident[:, :], compare_op=ALU.not_equal, fill=1.0,
                               base=0, pattern=[[-1, P]], channel_multiplier=1).then_inc(iota_made, 1)
            pool.memset(ones[:, :], 1.0).then_inc(iota_made, 1)
            for p in range(PASSES):
                table = (x, hv_d, xw_d)[p]
                if p > 0:
                    done = xw_out if p == ROUNDS else rows_out
                    pool.wait_ge(done[0], 16 * EVEN)
                    pool.wait_ge(done[1], 16 * ODD)
                with pool.Fori(0, ITERS) as i:
                    for s in range(SLOTS):
                        pool.wait_ge(idx_staged, i * SLOTS + (p * NG + s + 1))
                        pool.sem_inc(wait_over, 1)
                        pool.wait_ge(slot_free[p], i * SLOTS + (s + 1))
                        pool.sem_inc(wait_over, 1)
                        for t in range(G):
                            pool.indirect_dma_start(
                                msg[:, s, t, 0:H], None, table,
                                bass.IndirectOffsetOnAxis(idx_now[:, s, t:t + 1], 0)).then_inc(gathered[s], 16)

        @block.scalar
        def _(act):
            for p in range(PASSES):
                if p == 0:
                    act.wait_ge(src_in, 16)
                if p == ROUNDS:
                    act.wait_ge(relidx_in, 16)
                with act.Fori(0, ITERS) as i:
                    for s in range(SLOTS):
                        act.wait_ge(slot_free[p], i * SLOTS + (s + 1))
                        nc.scalar.copy(idx_now[:, s, :], srcidx[:, bass.ds((i * SLOTS + s) * G, G)])\
                          .then_inc(idx_staged, 1)
                if p == ROUNDS:
                    break
                n = p * CHUNKS
                last = p == ROUNDS - 1
                act.wait_ge(pass_done, p + 1)
                for step in chunk_steps(act, CHUNKS, 2):
                    if (k := step(0)):
                        c, b, h = k
                        wait(act, gates_made, c + (n - 1))
                        act.wait_ge(a_made, c + (n + 1))
                        nc.scalar.copy(a_t[b], pA[:, 0:C]).then_inc(a_copied, 1)
                    if (k := step(1)):
                        c, b, h = k
                        wait(act, hn_made, c + (n - 1))
                        act.wait_ge(gates_made, c + (n + 1))
                        nc.scalar.activation(r_t[b][0:H, :], pR[0:H, 0:C], ACT.Sigmoid).then_inc(rz_made, 1)
                        nc.scalar.activation(z_t[b][0:H, :], pR[H:2 * H, 0:C], ACT.Sigmoid).then_inc(rz_made, 1)
                        act.wait_ge(n_arg_made, c + (n + 1))
                        nc.scalar.activation(n_t[b][0:H, :], t_t[b][0:H, :], ACT.Tanh).then_inc(n_made, 1)
                    if (k := step(2)) and not last:
                        c, b, h = k
                        act.wait_ge(hn_made, c + (n + 1))
                        nc.scalar.copy(nodes[0:H, cols(c)], hn_t[b][0:H, :]).then_inc(hv_kept, 1)
                if not last:
                    continue
                act.wait_ge(var_made, 1)
                nc.scalar.activation(stdall[0:CP, :, :], varall[0:CP, :, :], ACT.Sqrt, scale=1.0 / H,
                                     bias=eps[0:CP, :]).then_inc(std_made, 1)
                for step in chunk_steps(act, CHUNKS, 1):
                    if (k := step(0)):
                        c, b, h = k
                        wait(act, xw_made, c * CJ - CJ)
                        act.wait_ge(y_turned, c + 1)
                        nc.scalar.copy(yT_t[b][0:H, :], pY[0:H, 0:C]).then_inc(yT_made, 1)
                    if (k := step(1)):
                        c, b, h = k
                        wait(act, xw_out[b], h * 16)
                        for j in (0, 1):
                            act.wait_ge(xw_made, c * CJ + (j + 1))
                            nc.scalar.copy(xw_t[b][0:CP, j * PAD:(j + 1) * PAD], pX[j][0:CP, :])\
                              .then_inc(xw_by_act, 1)
            act.wait_ge(pass_done, PASSES)
            for step in chunk_steps(act, CHUNKS, 1):
                if (k := step(0)):
                    c, b, h = k
                    wait(act, sums_turned, c - 1)
                    nc.scalar.copy(yT_t[b][0:H, :], sums[0:H, cols(c)]).then_inc(sums_copied, 1)
                if (k := step(1)):
                    c, b, h = k
                    act.wait_ge(var2_made, c + 1)
                    nc.scalar.activation(std[0:CP, b, :], var[0:CP, b, :], ACT.Sqrt, scale=1.0 / H,
                                         bias=eps[0:CP, :]).then_inc(std2_made, 1)

        @block.tensor
        def _(pe):
            pe.wait_ge(iota_made, 4)
            pe.wait_ge(lims_found, 2)
            nc.tensor.transpose(pS[0:NG, 0:P], lim[:, 0, :], ident[:, :]).then_inc(lims_turned, 1)
            nc.tensor.transpose(pS[0:NG, P:2 * P], lim[:, 1, :], ident[:, :]).then_inc(lims_turned, 1)
            pe.wait_ge(diag_made, 2)
            nc.tensor.matmul(pH[:, 0:2 * NG], ones[0:NG, :], diag[:, :, :].rearrange("p a b -> p (a b)"),
                             start=True, stop=True).then_inc(lims_spread, 1)
            pe.wait_ge(plan_made, 3)
            pe.wait_ge(memory_set, 5)
            pe.wait_ge(const_in, 16 * 7)
            pe.wait_ge(nodes_in, 16)
            for p in range(PASSES):
                features = H + 1 if p == 0 else H
                with pe.Fori(0, ITERS) as i:
                    for s in range(SLOTS):
                        g = i * SLOTS + s
                        windows = pe.value_load(plan[0:1, 1, bass.ds(g, 1)], min_val=1, max_val=P)
                        before = pe.value_load(plan[0:1, 2, bass.ds(g, 1)], min_val=0, max_val=NG * P)
                        pe.wait_ge(gathered[s], i * (16 * G) + (p * 16 * G * ITERS + 16 * G))
                        pe.sem_inc(wait_over, 1)
                        if p == 0:
                            pe.wait_ge(he_in[s % 2], i * (48 if s % 2 == 0 else 32) + 16 * (s // 2 + 1))
                            pe.sem_inc(wait_over, 1)
                        with pe.Fori(0, windows) as w:
                            pe.wait_ge(onehots_ready[p], before + w + 1)
                            pe.sem_inc(wait_over, 1)
                            for t in range(G):
                                done = nc.tensor.matmul(pS[0:features, 0:P], msg[:, s, t, 0:features], onehot[:, t, :],
                                                        start=t == 0, stop=t == G - 1)
                            if p == 0:
                                for t in range(G):
                                    done = nc.tensor.matmul(pH[H:2 * H, 0:P], he_t[:, s % 2, t * H:(t + 1) * H],
                                                            onehot[:, t, :], start=t == 0, stop=t == G - 1)
                            done.then_inc(window_summed[p], 1)
                if p == ROUNDS:
                    break
                n = p * CHUNKS
                last = p == ROUNDS - 1
                pe.wait_ge(pass_done, p + 1)
                for step in chunk_steps(pe, CHUNKS, 2):
                    if (k := step(0)):
                        c, b, h = k
                        wait(pe, dh_made, c + n)
                        nc.tensor.matmul(pD[0:H + 1, 0:C], wsel[:, :], nodes[:, cols(c)], start=True, stop=True)\
                          .then_inc(deg_spread, 1)
                        wait(pe, a_copied, c + n)
                        nc.tensor.matmul(pA[:, 0:C], wedge[:, p, :], sums[:, cols(c)], start=True, stop=False)
                        pe.wait_ge(dh_made, c + (n + 1))
                        nc.tensor.matmul(pA[:, 0:C], wdst[:, p, :], dh[b][0:H + 1, :], start=False, stop=True)\
                          .then_inc(a_made, 1)
                    if (k := step(1)):
                        c, b, h = k
                        wait(pe, rz_made, c * 2 + 2 * n)
                        nc.tensor.matmul(pR[:, 0:C], wnode[:, p, 0:P], nodes[:, cols(c)], start=True, stop=False)
                        wait(pe, n_arg_made, c + n)
                        nc.tensor.matmul(pN[:, 0:C], wnode[:, p, P:2 * P], nodes[:, cols(c)], start=True, stop=False)
                        pe.wait_ge(a_copied, c + (n + 1))
                        nc.tensor.matmul(pR[:, 0:C], wa[:, p, 0:P], a_t[b], start=False, stop=True)
                        nc.tensor.matmul(pN[:, 0:C], wa[:, p, P:2 * P], a_t[b], start=False, stop=True)\
                          .then_inc(gates_made, 1)
                    if (k := step(2)):
                        c, b, h = k
                        wait(pe, rows_read, c + n)
                        pe.wait_ge(hn_made, c + (n + 1))
                        pe.sem_inc(wait_over, 1)
                        hn_rows = hn_t[b][0:H, :].rearrange("f (p j) -> f j p", j=CJ)
                        for j in range(CJ):
                            turned = nc.tensor.transpose(pT[0:CP, j * H:(j + 1) * H], hn_rows[:, j, :], ident[0:H, 0:H])
                        turned.then_inc(hn_turned, 1)
                if not last:
                    continue
                for step in chunk_steps(pe, CHUNKS, 1):
                    if (k := step(0)):
                        c, b, h = k
                        wait(pe, yT_made, c)
                        pe.wait_ge(y_made, c + 1)
                        pe.sem_inc(wait_over, 1)
                        for j in range(CJ):
                            turned = nc.tensor.transpose(pY[0:H, j * CP:(j + 1) * CP], y_t[b][0:CP, j * H:(j + 1) * H],
                                                         ident[0:CP, 0:CP])
                        turned.then_inc(y_turned, 1)
                    if (k := step(1)):
                        c, b, h = k
                        pe.wait_ge(yT_made, c + 1)
                        pe.sem_inc(wait_over, 1)
                        for j in range(CJ):
                            wait(pe, xw_by_act if j < 2 else xw_by_dve, c * 2 + (j % 2 - 1))
                            nc.tensor.matmul(pX[j][0:CP, :], yT_t[b][0:H, j * CP:(j + 1) * CP], wrel[:, :],
                                             start=True, stop=True).then_inc(xw_made, 1)
            for step in chunk_steps(pe, CHUNKS, 0):
                c, b, h = step(0)
                wait(pe, turned_read, c)
                pe.wait_ge(sums_copied, c + 1)
                pe.sem_inc(wait_over, 1)
                y_rows = yT_t[b][0:H, :].rearrange("f (p j) -> f j p", j=CJ)
                for j in range(CJ):
                    turned = nc.tensor.transpose(pT[0:CP, j * H:(j + 1) * H], y_rows[:, j, :], ident[0:H, 0:H])
                turned.then_inc(sums_turned, 1)

        @block.vector
        def _(dve):
            steps = 0

            def chained(instruction):
                nonlocal steps
                steps += 1
                instruction.then_inc(dve_step, 1)
                dve.wait_ge(dve_step, steps)

            nc.vector.memset(msg[:, :, :, H:H + 1], 1.0).then_inc(slot_free[0], SLOTS)
            chained(nc.vector.memset(nodes[H:K_NODE, :], 1.0))
            nc.vector.memset(nodes[H:H + 1, :], 0.0).then_inc(memory_set, 1)
            nc.vector.memset(eps[:, :], EPS).then_inc(memory_set, 1)
            dve.wait_ge(dst_in, 16)
            chained(nc.vector.tensor_copy(dstrel[:, :, :].rearrange("p a b -> p (a b)"), dsti))
            nc.vector.tensor_reduce(lim[:, 0, :], dstrel[:, :, :], axis=AX.X, op=ALU.max).then_inc(lims_found, 1)
            nc.vector.tensor_reduce(lim[:, 1, :], dstrel[:, :, :], axis=AX.X, op=ALU.min, negate=True)\
              .then_inc(lims_found, 1)
            dve.wait_ge(src_in, 16)
            chained(nc.vector.tensor_scalar(relf, srcidx[:, :], float(RELS), None, op0=ALU.mult))
            dve.wait_ge(type_in, 16)
            nc.vector.tensor_tensor(relidx, relf, type_t, op=ALU.add).then_inc(relidx_made, 1)
            dve.wait_ge(lims_turned, 2)
            chained(nc.vector.tensor_reduce(limT[:, :], pS[0:NG, 0:2 * P].rearrange("p (a b) -> p a b", a=2),
                                            axis=AX.X, op=ALU.max))
            dve.wait_ge(iota_made, 4)
            for a in range(2):
                nc.vector.tensor_scalar(diag[:, a, :], ident[0:NG, 0:NG], limT[:, a:a + 1], None, op0=ALU.mult)\
                  .then_inc(diag_made, 1)
            dve.wait_ge(lims_spread, 1)
            greatest, neg_least = pH[:, 0:NG], pH[:, NG:2 * NG]
            nc.vector.tensor_scalar(plan[:, 0, :], neg_least, -1.0, None, op0=ALU.mult).then_inc(plan_made, 1)
            chained(nc.vector.tensor_copy(lim[:, 0, :], neg_least))
            nc.vector.tensor_tensor(dstrel[:, :, :], dstrel[:, :, :],
                                    lim[:, 0, :].unsqueeze(2).broadcast_to([P, NG, G]), op=ALU.add)
            chained(nc.vector.tensor_tensor(plan[:, 1, :], greatest, lim[:, 0, :], op=ALU.add))
            chained(nc.vector.tensor_scalar(plan[:, 1, :], plan[:, 1, :], P.bit_length() - 1, None,
                                            op0=ALU.arith_shift_right))
            chained(nc.vector.tensor_scalar(lim[:, 1, :], plan[:, 1, :], 1.0, None, op0=ALU.add))
            nc.vector.tensor_copy(plan[:, 1, :], lim[:, 1, :]).then_inc(plan_made, 1)
            chained(nc.vector.tensor_tensor_scan(lim[:, 0, :], ones[:, 0:NG], lim[:, 1, :], initial=0.0,
                                                 op0=ALU.mult, op1=ALU.add))
            nc.vector.tensor_tensor(plan[:, 2, :], lim[:, 0, :], lim[:, 1, :], op=ALU.subtract).then_inc(plan_made, 1)
            dve.wait_ge(relidx_out, 16)
            nc.vector.memset(sums[:, :], 0.0).then_inc(memory_set, 1)
            dve.wait_ge(plan_made, 3)
            dve.wait_ge(const_in, 16 * 7)
            dve.drain().then_inc(memory_set, 2)

            for p in range(PASSES):
                if p > 0:
                    dve.drain().then_inc(slot_free[p], SLOTS)
                with dve.Fori(0, ITERS) as i:
                    for s in range(SLOTS):
                        g = i * SLOTS + s
                        first = dve.value_load(plan[0:1, 0, bass.ds(g, 1)], min_val=0, max_val=N - 1)
                        windows = dve.value_load(plan[0:1, 1, bass.ds(g, 1)], min_val=1, max_val=P)
                        before = dve.value_load(plan[0:1, 2, bass.ds(g, 1)], min_val=0, max_val=NG * P)
                        nc.vector.tensor_copy(dst_now[:, :], dstrel[:, bass.ds(g, 1), :].rearrange("p a t -> p (a t)"))
                        if p == ROUNDS:
                            nc.vector.tensor_copy(ewt_now[:, :], ewt[:, bass.ds(g * G, G)])
                        with dve.Fori(0, windows) as w:
                            dve.drain()
                            for t in range(G):
                                if p == ROUNDS:
                                    made = nc.vector.tensor_scalar(onehot[:, t, :], iota[:, :], dst_now[:, t:t + 1],
                                                                   ewt_now[:, t:t + 1], op0=ALU.is_equal, op1=ALU.mult)
                                else:
                                    made = nc.vector.tensor_scalar(onehot[:, t, :], iota[:, :], dst_now[:, t:t + 1],
                                                                   None, op0=ALU.is_equal)
                            made.then_inc(onehots_ready[p], 1)
                            dve.wait_ge(window_summed[p], before + w + 1)
                            dve.sem_inc(wait_over, 1)
                            dve.drain()
                            nc.vector.tensor_scalar(dst_now[:, :], dst_now[:, :], -float(P), None, op0=ALU.add)
                            span = bass.ds(nc.s_assert_within(first + w * P, min_val=0, max_val=N - 1), P)
                            nc.vector.tensor_tensor(sums[0:H, span], sums[0:H, span], pS[0:H, 0:P], op=ALU.add)
                            if p == 0:
                                nc.vector.tensor_tensor(nodes[H:H + 1, span], nodes[H:H + 1, span],
                                                        pS[H:H + 1, 0:P], op=ALU.add)
                                nc.vector.tensor_tensor(sums[H:2 * H, span], sums[H:2 * H, span],
                                                        pH[H:2 * H, 0:P], op=ALU.add)
                        dve.drain()
                        dve.sem_inc(slot_free[p], 1)
                dve.drain().then_inc(pass_done, 1)
                if p == ROUNDS:
                    break
                last = p == ROUNDS - 1
                n = p * CHUNKS
                if last:
                    dve.wait_ge(resid_in, 16)
                for step in chunk_steps(dve, CHUNKS, 3):
                    if (k := step(0)):
                        c, b, h = k
                        wait(dve, a_made, c + (n - 1))
                        dve.wait_ge(deg_spread, c + (n + 1))
                        nc.vector.tensor_tensor(dh[b][0:H + 1, :], nodes[0:H + 1, cols(c)], pD[0:H + 1, 0:C],
                                                op=ALU.mult).then_inc(dh_made, 1)
                    if (k := step(1)):
                        c, b, h = k
                        dve.wait_ge(rz_made, c * 2 + (2 * n + 2))
                        nc.vector.tensor_tensor(t_t[b][0:H, :], r_t[b][0:H, :], pN[0:H, 0:C], op=ALU.mult)
                        dve.drain()
                        nc.vector.tensor_tensor(t_t[b][0:H, :], t_t[b][0:H, :], pN[H:2 * H, 0:C], op=ALU.add)\
                          .then_inc(n_arg_made, 1)
                    if (k := step(2)):
                        c, b, h = k
                        if not last:
                            wait(dve, hv_kept, c + (n - 1))
                        wait(dve, hn_turned, c + (n - 1))
                        dve.wait_ge(n_made, c + (n + 1))
                        nc.vector.tensor_tensor(t_t[b][0:H, :], nodes[0:H, cols(c)], n_t[b][0:H, :], op=ALU.subtract)
                        dve.drain()
                        nc.vector.tensor_tensor(t_t[b][0:H, :], t_t[b][0:H, :], z_t[b][0:H, :], op=ALU.mult)
                        dve.drain()
                        nc.vector.tensor_tensor(hn_t[b][0:H, :], n_t[b][0:H, :], t_t[b][0:H, :], op=ALU.add)\
                          .then_inc(hn_made, 1)
                    if (k := step(3)):
                        c, b, h = k
                        if not last:
                            wait(dve, rows_out[b], h * 16)
                            dve.wait_ge(hn_turned, c + (n + 1))
                            nc.vector.tensor_copy(nm[b][0:CP, :], pT[0:CP, 0:CJ * H]).then_inc(rows_read, 1)
                        else:
                            here = resid[0:CP, bass.ds(c, 1), :, :].rearrange("p a j f -> p (a j) f")
                            turned = pT[0:CP, 0:CJ * H].rearrange("p (j f) -> p j f", j=CJ)
                            dve.wait_ge(hn_turned, c + (n + 1))
                            nc.vector.tensor_tensor(here, here, turned, op=ALU.add).then_inc(rows_read, 1)
                            dve.drain()
                            nc.vector.tensor_reduce(mean[0:CP, b, :], here, axis=AX.X, op=ALU.add)
                            dve.drain()
                            nc.vector.tensor_scalar(mean[0:CP, b, :], mean[0:CP, b, :], -1.0 / H, None, op0=ALU.mult)
                            dve.drain()
                            nc.vector.tensor_tensor(here, here, mean[0:CP, b, :].unsqueeze(2).broadcast_to([CP, CJ, H]),
                                                    op=ALU.add)
                            dve.drain()
                            squares = sq[b][0:CP, :].rearrange("p (j f) -> p j f", j=CJ)
                            nc.vector.tensor_tensor(squares, here, here, op=ALU.mult)
                            dve.drain()
                            nc.vector.tensor_reduce(varall[0:CP, bass.ds(c, 1), :].rearrange("p a j -> p (a j)"),
                                                    squares, axis=AX.X, op=ALU.add)
                dve.wait_ge(a_made, n + CHUNKS)
                nc.vector.memset(sums[0:H, :], 0.0)
                if not last:
                    dve.wait_ge(hv_kept, n + CHUNKS)
                    dve.wait_ge(rows_out[0], 16 * EVEN)
                    dve.wait_ge(rows_out[1], 16 * ODD)
                    continue
                dve.drain().then_inc(var_made, 1)
                dve.wait_ge(std_made, 1)
                nc.vector.reciprocal(stdall[0:CP, :, :], stdall[0:CP, :, :])
                dve.drain()
                for step in chunk_steps(dve, CHUNKS, 1):
                    if (k := step(0)):
                        c, b, h = k
                        here = resid[0:CP, bass.ds(c, 1), :, :].rearrange("p a j f -> p (a j) f")
                        rstd = stdall[0:CP, bass.ds(c, 1), :].rearrange("p a j -> p (a j)")
                        wait(dve, y_out[b], h * 16)
                        wait(dve, y_turned, c - 1)
                        nc.vector.tensor_tensor(y_t[b][0:CP, :].rearrange("p (j f) -> p j f", j=CJ), here,
                                                rstd.unsqueeze(2).broadcast_to([CP, CJ, H]), op=ALU.mult)\
                          .then_inc(y_made, 1)
                    if (k := step(1)):
                        c, b, h = k
                        wait(dve, xw_out[b], h * 16)
                        for j in (2, 3):
                            dve.wait_ge(xw_made, c * CJ + (j + 1))
                            nc.vector.tensor_copy(xw_t[b][0:CP, j * PAD:(j + 1) * PAD], pX[j][0:CP, :])\
                              .then_inc(xw_by_dve, 1)
                dve.wait_ge(xw_by_act, 2 * CHUNKS)
                for b, many in ((0, EVEN), (1, ODD)):
                    dve.wait_ge(y_out[b], 16 * many)
                    dve.wait_ge(xw_out[b], 16 * many)
            dve.wait_ge(y_in, 16)
            for step in chunk_steps(dve, CHUNKS, 1):
                if (k := step(0)):
                    c, b, h = k
                    here = resid[0:CP, bass.ds(c, 1), :, :].rearrange("p a j f -> p (a j) f")
                    rows = y_t[b][0:CP, :].rearrange("p (j f) -> p j f", j=CJ)
                    squares = sq[b][0:CP, :].rearrange("p (j f) -> p j f", j=CJ)
                    dve.drain()
                    dve.wait_ge(sums_turned, c + 1)
                    nc.vector.tensor_tensor(rows, here, pT[0:CP, 0:CJ * H].rearrange("p (j f) -> p j f", j=CJ),
                                            op=ALU.add).then_inc(turned_read, 1)
                    dve.drain()
                    nc.vector.tensor_reduce(mean[0:CP, b, :], rows, axis=AX.X, op=ALU.add)
                    dve.drain()
                    nc.vector.tensor_scalar(mean[0:CP, b, :], mean[0:CP, b, :], -1.0 / H, None, op0=ALU.mult)
                    dve.drain()
                    nc.vector.tensor_tensor(rows, rows, mean[0:CP, b, :].unsqueeze(2).broadcast_to([CP, CJ, H]),
                                            op=ALU.add)
                    dve.drain()
                    nc.vector.tensor_tensor(squares, rows, rows, op=ALU.mult)
                    dve.drain()
                    nc.vector.tensor_reduce(var[0:CP, b, :], squares, axis=AX.X, op=ALU.add).then_inc(var2_made, 1)
                if (k := step(1)):
                    c, b, h = k
                    rows = y_t[b][0:CP, :].rearrange("p (j f) -> p j f", j=CJ)
                    wait(dve, fin_out[b], h * 16)
                    dve.wait_ge(std2_made, c + 1)
                    nc.vector.reciprocal(var[0:CP, b, :], std[0:CP, b, :])
                    dve.drain()
                    nc.vector.tensor_tensor(nm[b][0:CP, :].rearrange("p (j f) -> p j f", j=CJ), rows,
                                            var[0:CP, b, :].unsqueeze(2).broadcast_to([CP, CJ, H]), op=ALU.mult)\
                      .then_inc(fin_made, 1)


def kernel(x, src, dst, edge_attr_64, edge_type_8, edge_weight, L0_gnn_w_msg, L0_gnn_b_msg, L0_gnn_w_ih,
           L0_gnn_w_hh, L0_gnn_b_ih, L0_gnn_b_hh, L1_gnn_W):
    import numpy as np
    import concourse.bacc as bacc
    from concourse.bass_utils import run_bass_kernel_spmd

    R, H3, _ = L0_gnn_w_ih.shape
    H = H3 // 3

    def by_partition(a):
        return np.asarray(a).reshape(-1, P, G).transpose(1, 0, 2).reshape(P, -1)

    w_msg = np.asarray(L0_gnn_w_msg).transpose(2, 0, 1)
    w_ih = np.asarray(L0_gnn_w_ih).transpose(2, 0, 1)
    w_hh = np.asarray(L0_gnn_w_hh).transpose(2, 0, 1)
    b_ih, b_hh = np.asarray(L0_gnn_b_ih), np.asarray(L0_gnn_b_hh)
    w_node = np.zeros((H + 3, R, 4 * H), w_hh.dtype)
    w_node[:H, :, :H3] = w_hh
    w_node[H + 1, :, :H3] = b_hh
    w_node[H + 2, :, :2 * H] = b_ih[:, :2 * H]
    w_node[H + 2, :, H3:] = b_ih[:, 2 * H:]
    w_a = np.zeros((2 * H, R, 4 * H), w_ih.dtype)
    w_a[:, :, :2 * H] = w_ih[:, :, :2 * H]
    w_a[:, :, H3:] = w_ih[:, :, 2 * H:]
    w_sel = np.zeros((H + 3, H + 1), np.float32)
    w_sel[H, :H] = 1
    w_sel[H + 1, H] = 1
    arrays = {
        "x": np.asarray(x),
        "xT": np.asarray(x).T,
        "src": by_partition(src),
        "dst": by_partition(dst),
        "etype": by_partition(edge_type_8),
        "eweight": by_partition(edge_weight),
        "he": np.asarray(edge_attr_64),
        "w_edge": w_msg[H:],
        "w_dst": np.concatenate([w_msg[:H], np.asarray(L0_gnn_b_msg)[None]]),
        "w_node": w_node,
        "w_a": w_a,
        "w_sel": w_sel,
        "w_rel": np.asarray(L1_gnn_W).transpose(1, 0, 2).reshape(H, -1),
    }
    arrays = {f"in_{k}": np.ascontiguousarray(v) for k, v in arrays.items()}
    nc = bacc.Bacc("TRN2", target_bir_lowering=False, num_devices=1)
    args = [nc.dram_tensor(k, v.shape, mybir.dt.from_np(v.dtype), kind="ExternalInput").ap() for k, v in arrays.items()]
    out = nc.dram_tensor("out_rows", np.asarray(x).shape, F32, kind="ExternalOutput").ap()
    gnn_program(nc, *args, out)
    r = run_bass_kernel_spmd(nc, [arrays], core_ids=[0])
    return r.results[0]["out_rows"]
```

```python
from contextlib import ExitStack

import concourse.bass as bass
from concourse import mybir

F32 = mybir.dt.float32
I32 = mybir.dt.int32
ALU = mybir.AluOpType
ACT = mybir.ActivationFunctionType
AX = mybir.AxisListType

P = 128
G = 25
SLOTS = 5
PART = 5
W = 66
C = 500
CP, CJ = 125, 4
PAD = 512
EPS = 1e-5


def gnn_program(nc, x, xT, src, dst, etype, eweight, he, w_edge, w_dst, w_node, w_a, w_sel, w_rel, out):
    N, H = x.shape
    E = he.shape[0]
    ROUNDS = w_edge.shape[1]
    RELS = w_rel.shape[1] // H
    NG = E // (P * G)
    ITERS = NG // SLOTS
    CHUNKS = N // C
    NW = N + P
    PASSES = ROUNDS + 1
    K_NODE = H + 3
    assert NG * P * G == E and ITERS * SLOTS == NG and CHUNKS * C == N and H == 64 and CP * CJ == C

    he_v = he.rearrange("(g p t) f -> g p (t f)", p=P, t=G)
    x_v = x.rearrange("(c p j) f -> c p (j f)", p=CP, j=CJ)
    out_v = out.rearrange("(c p j) f -> c p (j f)", p=CP, j=CJ)
    hv_d = nc.dram_tensor("hv_d", [N, H], F32).ap()
    y_d = nc.dram_tensor("y_d", [N, H], F32).ap()
    xw_d = nc.dram_tensor("xw_d", [N * RELS, H], F32).ap()
    relidx_d = nc.dram_tensor("relidx_d", [P, NG * G], I32).ap()
    hv_v = hv_d.rearrange("(c p j) f -> c p (j f)", p=CP, j=CJ)
    y_v = y_d.rearrange("(c p j) f -> c p (j f)", p=CP, j=CJ)
    xw_v = xw_d.rearrange("(c p j r) f -> c p (j r f)", p=CP, j=CJ, r=RELS)

    ctx = ExitStack()
    with ctx:
        def sb(name, shape, dt=F32):
            return ctx.enter_context(nc.sbuf_tensor(name, shape, dt))

        def ps(name):
            return ctx.enter_context(nc.psum_tensor(name, [P, PAD], F32))

        def sem(name):
            return ctx.enter_context(nc.semaphore(name))

        sums = sb("sums", [P, NW])
        nodes = sb("nodes", [K_NODE, NW])
        srcidx = sb("srcidx", [P, NG * G], I32)
        dstrel = sb("dstrel", [P, NG, G])
        msg = sb("msg", [P, SLOTS, G, W])
        edge_area = sb("edge_area", [P, 2 * G * H])
        he_t = edge_area[:, :].rearrange("p (a f) -> p a f", a=2)
        ewt = edge_area[:, 0:NG * G]
        onehot = sb("onehot", [P, G, P])
        idx_now = sb("idx_now", [P, SLOTS, G], I32)
        dst_now = sb("dst_now", [P, G])
        ewt_now = sb("ewt_now", [P, G])
        iota = sb("iota", [P, P])
        ident = sb("ident", [P, P])
        ones = sb("ones", [P, P])
        lim = sb("lim", [P, 2, NG])
        limT = sb("limT", [NG, 2])
        diag = sb("diag", [NG, 2, NG])
        plan = sb("plan", [P, 3, NG], I32)
        wedge = sb("wedge", [P, ROUNDS, P])
        wdst = sb("wdst", [H + 1, ROUNDS, P])
        wnode = sb("wnode", [K_NODE, ROUNDS, 2 * P])
        wa = sb("wa", [P, ROUNDS, 2 * P])
        wsel = sb("wsel", [K_NODE, H + 1])
        wrel = sb("wrel", [H, RELS * H])
        eps = sb("eps", [P, 1])
        mean = sb("mean", [P, CJ])
        var = sb("var", [P, CJ])
        std = sb("std", [P, CJ])
        ready = sb("ready", [P, ITERS + 1], I32)
        limits = sb("limits", [P, CHUNKS])
        least = sb("least", [P, ITERS])

        dh, a_t, r_t, z_t, t_t = [sb(n, [P, C])[:, :] for n in ("dh", "a_t", "r_t", "z_t", "t_t")]
        n_t, hn_t = a_t, r_t
        nm = sb("nm", [P, CJ * H])[:, :]
        xw_t = edge_area[:, 0:CJ * RELS * H]
        o = CJ * RELS * H
        yT_t = edge_area[:, o:o + C]
        x_t = edge_area[:, o + C:o + C + CJ * H]
        sq = edge_area[:, o + C + CJ * H:o + C + 2 * CJ * H]
        assert o + C + 2 * CJ * H <= 2 * G * H and NG * G <= 2 * G * H
        yf_t, xf_t, rows_t, sqf = dh, a_t[:, 0:CJ * H], r_t[:, 0:CJ * H], z_t[:, 0:CJ * H]
        relf = sums[:, 0:NG * G]
        relidx = sums[:, NG * G:2 * NG * G].bitcast(I32)
        type_t = sums[:, 2 * NG * G:3 * NG * G].bitcast(I32)
        dsti = sums[:, 3 * NG * G:4 * NG * G].bitcast(I32)
        passed = sums[:, 0:ITERS * CHUNKS].rearrange("p (i c) -> p i c", c=CHUNKS)
        later = onehot[:, :, :].rearrange("p a b -> p (a b)")[:, 0:ITERS * NG].rearrange("p (i g) -> p i g", g=NG)

        pS, pH, pD, pA, pR, pN, pT, pI = [ps(n) for n in ("pS", "pH", "pD", "pA", "pR", "pN", "pT", "pI")]
        pY = pT
        numbers = pI[:, 0:P]
        pX = [pD, pA, pR, pN]

        const_in = sem("const_in")
        nodes_in = sem("nodes_in")
        src_in = sem("src_in")
        dst_in = sem("dst_in")
        type_in = sem("type_in")
        iota_made = sem("iota_made")
        memory_set = sem("memory_set")
        lims_found = sem("lims_found")
        lims_turned = sem("lims_turned")
        diag_made = sem("diag_made")
        lims_spread = sem("lims_spread")
        plan_made = sem("plan_made")
        dve_step = sem("dve_step")
        relidx_made = sem("relidx_made")
        relidx_out = sem("relidx_out")
        relidx_in = sem("relidx_in")
        ewt_in = sem("ewt_in")
        masks_made = sem("masks_made")
        he_in = [sem(f"he_in{n}") for n in range(2)]
        idx_staged = sem("idx_staged")
        gathered = [sem(f"gathered{n}") for n in range(SLOTS)]
        slot_free = [sem(f"slot_free{n}") for n in range(PASSES)]
        onehots_ready = [{t: sem(f"onehots_ready{n}_{t}") for t in range(0, G, PART)} for n in range(PASSES)]
        window_summed = [sem(f"window_summed{n}") for n in range(PASSES)]
        pass_done = sem("pass_done")
        step_done = sem("step_done")
        deg_spread = sem("deg_spread")
        dh_made = sem("dh_made")
        a_made = sem("a_made")
        a_copied = sem("a_copied")
        gates_made = sem("gates_made")
        rz_made = sem("rz_made")
        n_arg_made = sem("n_arg_made")
        n_made = sem("n_made")
        hn_made = sem("hn_made")
        hv_kept = sem("hv_kept")
        hn_turned = sem("hn_turned")
        rows_made = sem("rows_made")
        rows_out = sem("rows_out")
        x_in = sem("x_in")
        var_made = sem("var_made")
        std_made = sem("std_made")
        y_made = sem("y_made")
        y_turned = sem("y_turned")
        yT_made = sem("yT_made")
        y_out = sem("y_out")
        xw_made = sem("xw_made")
        xw_by_act = sem("xw_by_act")
        xw_by_dve = sem("xw_by_dve")
        xw_out = sem("xw_out")
        y_in = sem("y_in")
        sums_copied = sem("sums_copied")
        sums_turned = sem("sums_turned")
        var2_made = sem("var2_made")
        std2_made = sem("std2_made")
        fin_made = sem("fin_made")
        fin_out = sem("fin_out")
        wait_over = sem("wait_over")

        def cols(c):
            return bass.ds(c * C, C)

        def ready_chunks(eng, step, chunk):
            low = eng.value_load(ready[0:1, bass.ds(step, 1)], min_val=0, max_val=CHUNKS)
            high = eng.value_load(ready[0:1, bass.ds(step + 1, 1)], min_val=0, max_val=CHUNKS)
            with eng.If(low < high):
                with eng.Fori(low, high) as c:
                    chunk(nc.s_assert_within(c, min_val=0, max_val=CHUNKS - 1))
                eng.sem_inc(wait_over, 1)

        block = ctx.enter_context(nc.Block())

        @block.sync
        def _(sp):
            sp.dma_start(srcidx[:, :], src).then_inc(src_in, 16)
            sp.dma_start(dsti, dst).then_inc(dst_in, 16)
            sp.dma_start(wedge[:, :, :], w_edge).then_inc(const_in, 16)
            sp.dma_start(wdst[:, :, :], w_dst).then_inc(const_in, 16)
            sp.dma_start(wnode[:, :, :], w_node).then_inc(const_in, 16)
            sp.dma_start(wa[:, :, :], w_a).then_inc(const_in, 16)
            sp.dma_start(wsel[:, :], w_sel).then_inc(const_in, 16)
            sp.dma_start(wrel[:, :], w_rel).then_inc(const_in, 16)
            sp.dma_start(type_t, etype).then_inc(type_in, 16)
            sp.dma_start(nodes[0:H, 0:N], xT).then_inc(nodes_in, 16)
            sp.wait_ge(relidx_made, 1)
            sp.dma_start(relidx_d, relidx).then_inc(relidx_out, 16)
            with sp.Fori(0, ITERS) as i:
                for s in range(SLOTS):
                    sp.wait_ge(slot_free[0], i * SLOTS + (SLOTS, SLOTS, SLOTS + 1, SLOTS + 2, SLOTS + 3)[s])
                    sp.sem_inc(wait_over, 1)
                    sp.dma_start(he_t[:, s % 2, :],
                                 he_v[bass.ds(i * SLOTS + s, 1), :, :].rearrange("a p f -> p (a f)"))\
                      .then_inc(he_in[s % 2], 16)
            sp.wait_ge(idx_staged, ROUNDS * NG)
            sp.wait_ge(relidx_out, 16)
            sp.dma_start(srcidx[:, :], relidx_d).then_inc(relidx_in, 16)
            sp.wait_ge(pass_done, ROUNDS)
            sp.wait_ge(xw_out, 16 * CHUNKS)
            sp.dma_start(ewt, eweight).then_inc(ewt_in, 16)
            sp.wait_ge(fin_out, 16 * CHUNKS)

        @block.gpsimd
        def _(pool):
            pool.iota(iota[:, :], [[1, P]], base=0, channel_multiplier=0,
                      allow_small_or_imprecise_dtypes=True).then_inc(iota_made, 1)
            pool.memset(ident[:, :], 0.0).then_inc(iota_made, 1)
            pool.wait_ge(iota_made, 2)
            pool.affine_select(out=ident[:, :], in_=ident[:, :], compare_op=ALU.not_equal, fill=1.0,
                               base=0, pattern=[[-1, P]], channel_multiplier=1).then_inc(iota_made, 1)
            pool.memset(ones[:, :], 1.0).then_inc(iota_made, 1)
            pool.memset(later, 0.0).then_inc(masks_made, 1)
            pool.iota(limits[:, :], [[C, CHUNKS]], base=C, channel_multiplier=0,
                      allow_small_or_imprecise_dtypes=True).then_inc(masks_made, 1)
            pool.wait_ge(masks_made, 2)
            pool.affine_select(out=later, in_=later, compare_op=ALU.is_ge, fill=float(N), base=-SLOTS,
                               pattern=[[-SLOTS, ITERS], [1, NG]], channel_multiplier=0).then_inc(masks_made, 1)
            for p in range(PASSES):
                table = (x, hv_d, xw_d)[p]
                if p > 0:
                    pool.wait_ge(xw_out if p == ROUNDS else rows_out, 16 * CHUNKS)
                with pool.Fori(0, ITERS) as i:
                    for s in range(SLOTS):
                        pool.wait_ge(idx_staged, i * SLOTS + (p * NG + s + 1))
                        pool.sem_inc(wait_over, 1)
                        pool.wait_ge(slot_free[p], i * SLOTS + (s + 1))
                        pool.sem_inc(wait_over, 1)
                        for t in range(G):
                            pool.indirect_dma_start(
                                msg[:, s, t, 0:H], None, table,
                                bass.IndirectOffsetOnAxis(idx_now[:, s, t:t + 1], 0)).then_inc(gathered[s], 16)

        @block.scalar
        def _(act):
            for p in range(PASSES):
                n = p * CHUNKS
                last = p == ROUNDS - 1

                def gru_chunk(c):
                    if last:
                        act.dma_start(x_t[0:CP, :], x_v[bass.ds(c, 1), :, :].rearrange("a p f -> p (a f)"))\
                           .then_inc(x_in, 16)
                    act.wait_ge(a_made, c + (n + 1))
                    nc.scalar.copy(a_t, pA[:, 0:C]).then_inc(a_copied, 1)
                    act.wait_ge(gates_made, c + (n + 1))
                    nc.scalar.activation(r_t[0:H, :], pR[0:H, 0:C], ACT.Sigmoid).then_inc(rz_made, 1)
                    nc.scalar.activation(z_t[0:H, :], pR[H:2 * H, 0:C], ACT.Sigmoid).then_inc(rz_made, 1)
                    act.wait_ge(n_arg_made, c + (n + 1))
                    nc.scalar.activation(n_t[0:H, :], t_t[0:H, :], ACT.Tanh).then_inc(n_made, 1)
                    if not last:
                        act.wait_ge(hn_made, c + (n + 1))
                        nc.scalar.copy(nodes[0:H, cols(c)], hn_t[0:H, :]).then_inc(hv_kept, 1)
                        act.wait_ge(rows_made, c + (n + 1))
                        act.dma_start(hv_v[bass.ds(c, 1), :, :].rearrange("a p f -> p (a f)"), nm[0:CP, :])\
                           .then_inc(rows_out, 16)
                        act.wait_ge(rows_out, c * 16 + (16 * n + 16))
                        return
                    act.wait_ge(var_made, c + 1)
                    nc.scalar.activation(std[0:CP, :], var[0:CP, :], ACT.Sqrt, scale=1.0 / H,
                                         bias=eps[0:CP, :]).then_inc(std_made, 1)
                    act.wait_ge(y_made, c + 1)
                    act.dma_start(y_v[bass.ds(c, 1), :, :].rearrange("a p f -> p (a f)"), nm[0:CP, :])\
                       .then_inc(y_out, 16)
                    act.wait_ge(y_turned, c + 1)
                    nc.scalar.copy(yT_t[0:H, :], pY[0:H, 0:C]).then_inc(yT_made, 1)
                    for j in (0, 1):
                        act.wait_ge(xw_made, c * CJ + (j + 1))
                        nc.scalar.copy(xw_t[0:CP, j * PAD:(j + 1) * PAD], pX[j][0:CP, :]).then_inc(xw_by_act, 1)
                    act.wait_ge(xw_by_act, c * 2 + 2)
                    act.sem_inc(wait_over, 1)
                    act.wait_ge(xw_by_dve, c * 2 + 2)
                    act.dma_start(xw_v[bass.ds(c, 1), :, :].rearrange("a p f -> p (a f)"), xw_t[0:CP, :])\
                       .then_inc(xw_out, 16)
                    act.wait_ge(y_out, c * 16 + 16)
                    act.sem_inc(wait_over, 1)
                    act.wait_ge(xw_out, c * 16 + 16)

                def final_chunk(c):
                    act.dma_start(xf_t[0:CP, :], y_v[bass.ds(c, 1), :, :].rearrange("a p f -> p (a f)"))\
                       .then_inc(y_in, 16)
                    nc.scalar.copy(yf_t[0:H, :], sums[0:H, cols(c)]).then_inc(sums_copied, 1)
                    act.wait_ge(var2_made, c + 1)
                    nc.scalar.activation(std[0:CP, :], var[0:CP, :], ACT.Sqrt, scale=1.0 / H,
                                         bias=eps[0:CP, :]).then_inc(std2_made, 1)
                    act.wait_ge(fin_made, c + 1)
                    act.dma_start(out_v[bass.ds(c, 1), :, :].rearrange("a p f -> p (a f)"), nm[0:CP, :])\
                       .then_inc(fin_out, 16)
                    act.wait_ge(fin_out, c * 16 + 16)

                def chunk(c):
                    (final_chunk if p == ROUNDS else gru_chunk)(c)
                    act.sem_inc(wait_over, 1)

                if p == 0:
                    act.wait_ge(src_in, 16)
                    for s in range(SLOTS):
                        nc.scalar.copy(idx_now[:, s, :], srcidx[:, s * G:(s + 1) * G]).then_inc(idx_staged, 1)
                    act.wait_ge(plan_made, 5)
                with act.Fori(0, ITERS - 1) as i:
                    for s in range(SLOTS):
                        act.wait_ge(slot_free[p], i * SLOTS + (SLOTS + s + 1))
                        nc.scalar.copy(idx_now[:, s, :], srcidx[:, bass.ds((i * SLOTS + (SLOTS + s)) * G, G)])\
                          .then_inc(idx_staged, 1)
                    if p == ROUNDS:
                        act.wait_ge(step_done, i + (p * ITERS + 1))
                        act.sem_inc(wait_over, 1)
                    ready_chunks(act, i, chunk)
                if p < ROUNDS:
                    if p + 1 == ROUNDS:
                        act.wait_ge(relidx_in, 16)
                    for s in range(SLOTS):
                        act.wait_ge(slot_free[p], NG + s + 1)
                        nc.scalar.copy(idx_now[:, s, :], srcidx[:, s * G:(s + 1) * G]).then_inc(idx_staged, 1)
                act.wait_ge(step_done, (p + 1) * ITERS)
                ready_chunks(act, ITERS - 1, chunk)

        @block.tensor
        def _(pe):
            pe.wait_ge(iota_made, 4)
            pe.wait_ge(lims_found, 2)
            nc.tensor.transpose(pS[0:NG, 0:P], lim[:, 0, :], ident[:, :]).then_inc(lims_turned, 1)
            nc.tensor.transpose(pS[0:NG, P:2 * P], lim[:, 1, :], ident[:, :]).then_inc(lims_turned, 1)
            pe.wait_ge(diag_made, 2)
            nc.tensor.matmul(pH[:, 0:2 * NG], ones[0:NG, :], diag[:, :, :].rearrange("p a b -> p (a b)"),
                             start=True, stop=True).then_inc(lims_spread, 1)
            pe.wait_ge(plan_made, 5)
            pe.wait_ge(memory_set, 5)
            pe.wait_ge(const_in, 16 * 6)
            pe.wait_ge(nodes_in, 16)
            for p in range(PASSES):
                n = p * CHUNKS
                last = p == ROUNDS - 1

                def gru_chunk(c):
                    nc.tensor.matmul(pD[0:H + 1, 0:C], wsel[:, :], nodes[:, cols(c)], start=True, stop=True)\
                      .then_inc(deg_spread, 1)
                    nc.tensor.matmul(pA[:, 0:C], wedge[:, p, :], sums[:, cols(c)], start=True, stop=False)
                    nc.tensor.matmul(pR[:, 0:C], wnode[:, p, 0:P], nodes[:, cols(c)], start=True, stop=False)
                    nc.tensor.matmul(pN[:, 0:C], wnode[:, p, P:2 * P], nodes[:, cols(c)], start=True, stop=False)
                    pe.wait_ge(dh_made, c + (n + 1))
                    nc.tensor.matmul(pA[:, 0:C], wdst[:, p, :], dh[0:H + 1, :], start=False, stop=True)\
                      .then_inc(a_made, 1)
                    pe.wait_ge(a_copied, c + (n + 1))
                    nc.tensor.matmul(pR[:, 0:C], wa[:, p, 0:P], a_t, start=False, stop=True)
                    nc.tensor.matmul(pN[:, 0:C], wa[:, p, P:2 * P], a_t, start=False, stop=True)\
                      .then_inc(gates_made, 1)
                    pe.wait_ge(hn_made, c + (n + 1))
                    pe.sem_inc(wait_over, 1)
                    hn_rows = hn_t[0:H, :].rearrange("f (p j) -> f j p", j=CJ)
                    for j in range(CJ):
                        turned = nc.tensor.transpose(pT[0:CP, j * H:(j + 1) * H], hn_rows[:, j, :], ident[0:H, 0:H])
                    turned.then_inc(hn_turned, 1)
                    if not last:
                        return
                    pe.wait_ge(y_made, c + 1)
                    pe.sem_inc(wait_over, 1)
                    for j in range(CJ):
                        turned = nc.tensor.transpose(pY[0:H, j * CP:(j + 1) * CP], nm[0:CP, j * H:(j + 1) * H],
                                                     ident[0:CP, 0:CP])
                    turned.then_inc(y_turned, 1)
                    pe.wait_ge(yT_made, c + 1)
                    pe.sem_inc(wait_over, 1)
                    for j in range(CJ):
                        nc.tensor.matmul(pX[j][0:CP, :], yT_t[0:H, j * CP:(j + 1) * CP], wrel[:, :],
                                         start=True, stop=True).then_inc(xw_made, 1)
                    pe.wait_ge(xw_by_act, c * 2 + 2)
                    pe.sem_inc(wait_over, 1)
                    pe.wait_ge(xw_by_dve, c * 2 + 2)
                    pe.sem_inc(wait_over, 1)

                def final_chunk(c):
                    pe.wait_ge(sums_copied, c + 1)
                    pe.sem_inc(wait_over, 1)
                    y_rows = yf_t[0:H, :].rearrange("f (p j) -> f j p", j=CJ)
                    for j in range(CJ):
                        turned = nc.tensor.transpose(pT[0:CP, j * H:(j + 1) * H], y_rows[:, j, :], ident[0:H, 0:H])
                    turned.then_inc(sums_turned, 1)

                features = H + 1 if p == 0 else H
                with pe.Fori(0, ITERS) as i:
                    for s in range(SLOTS):
                        g = i * SLOTS + s
                        windows = pe.value_load(plan[0:1, 1, bass.ds(g, 1)], min_val=1, max_val=P)
                        before = pe.value_load(plan[0:1, 2, bass.ds(g, 1)], min_val=0, max_val=NG * P)
                        pe.wait_ge(gathered[s], i * (16 * G) + (p * 16 * G * ITERS + 16 * G))
                        pe.sem_inc(wait_over, 1)
                        if p == 0:
                            pe.wait_ge(he_in[s % 2], i * (48 if s % 2 == 0 else 32) + 16 * (s // 2 + 1))
                            pe.sem_inc(wait_over, 1)
                        with pe.Fori(0, windows) as w:
                            for t in range(G):
                                if t % PART == 0:
                                    pe.wait_ge(onehots_ready[p][t], before + w + 1)
                                    pe.sem_inc(wait_over, 1)
                                done = nc.tensor.matmul(pS[0:features, 0:P], msg[:, s, t, 0:features], onehot[:, t, :],
                                                        start=t == 0, stop=t == G - 1)
                            if p == 0:
                                for t in range(G):
                                    done = nc.tensor.matmul(pH[H:2 * H, 0:P], he_t[:, s % 2, t * H:(t + 1) * H],
                                                            onehot[:, t, :], start=t == 0, stop=t == G - 1)
                            done.then_inc(window_summed[p], 1)
                    pe.wait_ge(step_done, i + (p * ITERS + 1))
                    pe.sem_inc(wait_over, 1)
                    ready_chunks(pe, i, final_chunk if p == ROUNDS else gru_chunk)

        @block.vector
        def _(dve):
            steps = 0

            def chained(instruction):
                nonlocal steps
                steps += 1
                instruction.then_inc(dve_step, 1)
                dve.wait_ge(dve_step, steps)

            nc.vector.memset(msg[:, :, :, H:H + 1], 1.0).then_inc(slot_free[0], SLOTS)
            chained(nc.vector.memset(nodes[H:K_NODE, :], 1.0))
            nc.vector.memset(nodes[H:H + 1, :], 0.0).then_inc(memory_set, 1)
            nc.vector.memset(eps[:, :], EPS).then_inc(memory_set, 1)
            dve.wait_ge(iota_made, 4)
            nc.vector.tensor_copy(numbers, iota[:, :])
            dve.wait_ge(dst_in, 16)
            chained(nc.vector.tensor_copy(dstrel[:, :, :].rearrange("p a b -> p (a b)"), dsti))
            nc.vector.tensor_reduce(lim[:, 0, :], dstrel[:, :, :], axis=AX.X, op=ALU.max).then_inc(lims_found, 1)
            nc.vector.tensor_reduce(lim[:, 1, :], dstrel[:, :, :], axis=AX.X, op=ALU.min, negate=True)\
              .then_inc(lims_found, 1)
            dve.wait_ge(src_in, 16)
            chained(nc.vector.tensor_scalar(relf, srcidx[:, :], float(RELS), None, op0=ALU.mult))
            dve.wait_ge(type_in, 16)
            nc.vector.tensor_tensor(relidx, relf, type_t, op=ALU.add).then_inc(relidx_made, 1)
            dve.wait_ge(lims_turned, 2)
            chained(nc.vector.tensor_reduce(limT[:, :], pS[0:NG, 0:2 * P].rearrange("p (a b) -> p a b", a=2),
                                            axis=AX.X, op=ALU.max))
            for a in range(2):
                nc.vector.tensor_scalar(diag[:, a, :], ident[0:NG, 0:NG], limT[:, a:a + 1], None, op0=ALU.mult)\
                  .then_inc(diag_made, 1)
            dve.wait_ge(lims_spread, 1)
            greatest, neg_least = pH[:, 0:NG], pH[:, NG:2 * NG]
            nc.vector.tensor_scalar(plan[:, 0, :], neg_least, -1.0, None, op0=ALU.mult).then_inc(plan_made, 1)
            chained(nc.vector.tensor_copy(lim[:, 0, :], neg_least))
            nc.vector.tensor_tensor(dstrel[:, :, :], dstrel[:, :, :],
                                    lim[:, 0, :].unsqueeze(2).broadcast_to([P, NG, G]), op=ALU.add)
            chained(nc.vector.tensor_tensor(plan[:, 1, :], greatest, lim[:, 0, :], op=ALU.add))
            chained(nc.vector.tensor_scalar(plan[:, 1, :], plan[:, 1, :], P.bit_length() - 1, None,
                                            op0=ALU.arith_shift_right))
            chained(nc.vector.tensor_scalar(lim[:, 1, :], plan[:, 1, :], 1.0, None, op0=ALU.add))
            nc.vector.tensor_copy(plan[:, 1, :], lim[:, 1, :]).then_inc(plan_made, 1)
            chained(nc.vector.tensor_tensor_scan(lim[:, 0, :], ones[:, 0:NG], lim[:, 1, :], initial=0.0,
                                                 op0=ALU.mult, op1=ALU.add))
            nc.vector.tensor_tensor(plan[:, 2, :], lim[:, 0, :], lim[:, 1, :], op=ALU.subtract).then_inc(plan_made, 1)
            dve.drain()
            chained(nc.vector.tensor_copy(lim[:, 1, :], plan[:, 0, :]))
            dve.wait_ge(masks_made, 3)
            chained(nc.vector.tensor_tensor(later, later, lim[:, 1, :].unsqueeze(1).broadcast_to([P, ITERS, NG]),
                                            op=ALU.max))
            chained(nc.vector.tensor_reduce(least[:, :], later, axis=AX.X, op=ALU.min))
            chained(nc.vector.tensor_tensor(passed, least[:, :].unsqueeze(2).broadcast_to([P, ITERS, CHUNKS]),
                                            limits[:, :].unsqueeze(1).broadcast_to([P, ITERS, CHUNKS]), op=ALU.is_ge))
            chained(nc.vector.tensor_reduce(least[:, :], passed, axis=AX.X, op=ALU.add))
            nc.vector.tensor_copy(ready[:, 1:ITERS + 1], least[:, :]).then_inc(plan_made, 1)
            nc.vector.memset(ready[:, 0:1], 0).then_inc(plan_made, 1)
            dve.wait_ge(relidx_out, 16)
            nc.vector.memset(sums[:, :], 0.0).then_inc(memory_set, 1)
            dve.wait_ge(plan_made, 5)
            dve.wait_ge(const_in, 16 * 6)
            dve.wait_ge(nodes_in, 16)
            dve.drain().then_inc(memory_set, 2)

            for p in range(PASSES):
                n = p * CHUNKS
                last = p == ROUNDS - 1

                def gru_chunk(c):
                    dve.wait_ge(deg_spread, c + (n + 1))
                    nc.vector.tensor_tensor(dh[0:H + 1, :], nodes[0:H + 1, cols(c)], pD[0:H + 1, 0:C],
                                            op=ALU.mult).then_inc(dh_made, 1)
                    dve.wait_ge(rz_made, c * 2 + (2 * n + 2))
                    nc.vector.tensor_tensor(t_t[0:H, :], r_t[0:H, :], pN[0:H, 0:C], op=ALU.mult)
                    dve.drain()
                    nc.vector.tensor_tensor(t_t[0:H, :], t_t[0:H, :], pN[H:2 * H, 0:C], op=ALU.add)\
                      .then_inc(n_arg_made, 1)
                    dve.wait_ge(n_made, c + (n + 1))
                    nc.vector.tensor_tensor(t_t[0:H, :], nodes[0:H, cols(c)], n_t[0:H, :], op=ALU.subtract)
                    dve.drain()
                    nc.vector.tensor_tensor(t_t[0:H, :], t_t[0:H, :], z_t[0:H, :], op=ALU.mult)
                    dve.drain()
                    nc.vector.tensor_tensor(hn_t[0:H, :], n_t[0:H, :], t_t[0:H, :], op=ALU.add)\
                      .then_inc(hn_made, 1)
                    dve.wait_ge(hn_turned, c + (n + 1))
                    if not last:
                        nc.vector.tensor_copy(nm[0:CP, :], pT[0:CP, 0:CJ * H]).then_inc(rows_made, 1)
                        return
                    dve.sem_inc(wait_over, 1)
                    dve.wait_ge(x_in, c * 16 + 16)
                    norm_rows(x_t, x_t, sq, c, var_made, std_made).then_inc(y_made, 1)
                    for j in (2, 3):
                        dve.wait_ge(xw_made, c * CJ + (j + 1))
                        nc.vector.tensor_copy(xw_t[0:CP, j * PAD:(j + 1) * PAD], pX[j][0:CP, :])\
                          .then_inc(xw_by_dve, 1)

                def norm_rows(x_rows, sum_rows, square_rows, c, var_ready, std_ready):
                    rows, squares, result, turned = [
                        a[0:CP, 0:CJ * H].rearrange("p (j f) -> p j f", j=CJ) for a in (sum_rows, square_rows, nm, pT)]
                    old = x_rows[0:CP, :].rearrange("p (j f) -> p j f", j=CJ)
                    nc.vector.tensor_tensor(rows, old, turned, op=ALU.add)
                    dve.drain()
                    nc.vector.tensor_reduce(mean[0:CP, :], rows, axis=AX.X, op=ALU.add)
                    dve.drain()
                    nc.vector.tensor_scalar(mean[0:CP, :], mean[0:CP, :], -1.0 / H, None, op0=ALU.mult)
                    dve.drain()
                    nc.vector.tensor_tensor(rows, rows, mean[0:CP, :].unsqueeze(2).broadcast_to([CP, CJ, H]), op=ALU.add)
                    dve.drain()
                    nc.vector.tensor_tensor(squares, rows, rows, op=ALU.mult)
                    dve.drain()
                    nc.vector.tensor_reduce(var[0:CP, :], squares, axis=AX.X, op=ALU.add).then_inc(var_ready, 1)
                    dve.wait_ge(std_ready, c + 1)
                    nc.vector.reciprocal(mean[0:CP, :], std[0:CP, :])
                    dve.drain()
                    return nc.vector.tensor_tensor(result, rows, mean[0:CP, :].unsqueeze(2).broadcast_to([CP, CJ, H]),
                                                   op=ALU.mult)

                def final_chunk(c):
                    dve.wait_ge(sums_turned, c + 1)
                    dve.sem_inc(wait_over, 1)
                    dve.wait_ge(y_in, c * 16 + 16)
                    norm_rows(xf_t, rows_t, sqf, c, var2_made, std2_made).then_inc(fin_made, 1)

                if p > 0:
                    dve.drain().then_inc(slot_free[p], SLOTS)
                    nc.vector.memset(sums[0:H, :], 0.0)
                if p == ROUNDS:
                    dve.wait_ge(ewt_in, 16)
                with dve.Fori(0, ITERS) as i:
                    for s in range(SLOTS):
                        g = i * SLOTS + s
                        first = dve.value_load(plan[0:1, 0, bass.ds(g, 1)], min_val=0, max_val=N - 1)
                        windows = dve.value_load(plan[0:1, 1, bass.ds(g, 1)], min_val=1, max_val=P)
                        before = dve.value_load(plan[0:1, 2, bass.ds(g, 1)], min_val=0, max_val=NG * P)
                        nc.vector.tensor_copy(dst_now[:, :], dstrel[:, bass.ds(g, 1), :].rearrange("p a t -> p (a t)"))
                        if p == ROUNDS:
                            nc.vector.tensor_copy(ewt_now[:, :], edge_area[:, bass.ds(g * G, G)])
                        with dve.Fori(0, windows) as w:
                            dve.drain()
                            for t in range(G):
                                if p == ROUNDS:
                                    made = nc.vector.tensor_scalar(onehot[:, t, :], numbers, dst_now[:, t:t + 1],
                                                                   ewt_now[:, t:t + 1], op0=ALU.is_equal, op1=ALU.mult)
                                else:
                                    made = nc.vector.tensor_scalar(onehot[:, t, :], numbers, dst_now[:, t:t + 1],
                                                                   None, op0=ALU.is_equal)
                                if t % PART == PART - 1:
                                    made.then_inc(onehots_ready[p][t - PART + 1], 1)
                            dve.wait_ge(window_summed[p], before + w + 1)
                            dve.sem_inc(wait_over, 1)
                            dve.drain()
                            nc.vector.tensor_scalar(dst_now[:, :], dst_now[:, :], -float(P), None, op0=ALU.add)
                            span = bass.ds(nc.s_assert_within(first + w * P, min_val=0, max_val=N - 1), P)
                            nc.vector.tensor_tensor(sums[0:H, span], sums[0:H, span], pS[0:H, 0:P], op=ALU.add)
                            if p == 0:
                                nc.vector.tensor_tensor(nodes[H:H + 1, span], nodes[H:H + 1, span],
                                                        pS[H:H + 1, 0:P], op=ALU.add)
                                nc.vector.tensor_tensor(sums[H:2 * H, span], sums[H:2 * H, span],
                                                        pH[H:2 * H, 0:P], op=ALU.add)
                        dve.drain()
                        dve.sem_inc(slot_free[p], 1)
                    dve.drain().then_inc(step_done, 1)
                    ready_chunks(dve, i, final_chunk if p == ROUNDS else gru_chunk)
                dve.drain().then_inc(pass_done, 1)


def kernel(x, src, dst, edge_attr_64, edge_type_8, edge_weight, L0_gnn_w_msg, L0_gnn_b_msg, L0_gnn_w_ih,
           L0_gnn_w_hh, L0_gnn_b_ih, L0_gnn_b_hh, L1_gnn_W):
    import numpy as np
    import concourse.bacc as bacc
    from concourse.bass_utils import run_bass_kernel_spmd

    R, H3, _ = L0_gnn_w_ih.shape
    H = H3 // 3

    def by_partition(a):
        return np.asarray(a).reshape(-1, P, G).transpose(1, 0, 2).reshape(P, -1)

    w_msg = np.asarray(L0_gnn_w_msg).transpose(2, 0, 1)
    w_ih = np.asarray(L0_gnn_w_ih).transpose(2, 0, 1)
    w_hh = np.asarray(L0_gnn_w_hh).transpose(2, 0, 1)
    b_ih, b_hh = np.asarray(L0_gnn_b_ih), np.asarray(L0_gnn_b_hh)
    w_node = np.zeros((H + 3, R, 4 * H), w_hh.dtype)
    w_node[:H, :, :H3] = w_hh
    w_node[H + 1, :, :H3] = b_hh
    w_node[H + 2, :, :2 * H] = b_ih[:, :2 * H]
    w_node[H + 2, :, H3:] = b_ih[:, 2 * H:]
    w_a = np.zeros((2 * H, R, 4 * H), w_ih.dtype)
    w_a[:, :, :2 * H] = w_ih[:, :, :2 * H]
    w_a[:, :, H3:] = w_ih[:, :, 2 * H:]
    w_sel = np.zeros((H + 3, H + 1), np.float32)
    w_sel[H, :H] = 1
    w_sel[H + 1, H] = 1
    arrays = {
        "x": np.asarray(x),
        "xT": np.asarray(x).T,
        "src": by_partition(src),
        "dst": by_partition(dst),
        "etype": by_partition(edge_type_8),
        "eweight": by_partition(edge_weight),
        "he": np.asarray(edge_attr_64),
        "w_edge": w_msg[H:],
        "w_dst": np.concatenate([w_msg[:H], np.asarray(L0_gnn_b_msg)[None]]),
        "w_node": w_node,
        "w_a": w_a,
        "w_sel": w_sel,
        "w_rel": np.asarray(L1_gnn_W).transpose(1, 0, 2).reshape(H, -1),
    }
    arrays = {f"in_{k}": np.ascontiguousarray(v) for k, v in arrays.items()}
    nc = bacc.Bacc("TRN2", target_bir_lowering=False, num_devices=1)
    args = [nc.dram_tensor(k, v.shape, mybir.dt.from_np(v.dtype), kind="ExternalInput").ap() for k, v in arrays.items()]
    out = nc.dram_tensor("out_rows", np.asarray(x).shape, F32, kind="ExternalOutput").ap()
    gnn_program(nc, *args, out)
    r = run_bass_kernel_spmd(nc, [arrays], core_ids=[0])
    return r.results[0]["out_rows"]
```
